# Optimizing a Trainium2 kernel written in Bass

```python
import numpy as np
import jax
import jax.numpy as jnp

def _softmax(x, axis=-1):
    return jax.nn.softmax(x, axis=axis)

def _gelu(x):
    return jax.nn.gelu(x, approximate=True)

def _silu(x):
    return jax.nn.silu(x)

def _sigmoid(x):
    return jax.nn.sigmoid(x)

def _layernorm(x, axis=-1, eps=1e-05):
    m = jnp.mean(x, axis=axis, keepdims=True)
    v = jnp.var(x, axis=axis, keepdims=True)
    return (x - m) / jnp.sqrt(v + eps)

def _scatter_add(tgt, idx, src, axis=0):
    return tgt.at[idx].add(src)

def _segment_sum(src, seg, n):
    return jax.ops.segment_sum(src, seg, n)
kernel_name = 'mk_xattn_seq_d1_seqx_r4_2f29ba'

def setup_inputs(seed: int=0):
    np.random.seed(seed)
    _w = jnp.asarray

    def _rec_inputs():
        import jax
        import jax.numpy as jnp
        _rk = jax.random.key(seed)
        x = -0.0002928 + 1 * jax.random.normal(jax.random.fold_in(_rk, 1), (8, 256, 512), jnp.float32)
        _lenS = 256 - jax.random.randint(jax.random.fold_in(_rk, 7), (8,), 0, max(1, 256 // 4) + 1, jnp.int32)
        _lenS2 = 256 - jax.random.randint(jax.random.fold_in(_rk, 8), (8,), 0, max(1, 256 // 4) + 1, jnp.int32)
        _ctx_2048P = jax.random.normal(jax.random.fold_in(_rk, 11), (8, 16, 512), jnp.float32)
        _ctx_2048c = jax.random.dirichlet(jax.random.fold_in(_rk, 511), 0.3 * jnp.ones((16,), jnp.float32), (8, 256))
        _ctx_2048t = jnp.einsum('bsk,bkd->bsd', _ctx_2048c, _ctx_2048P)
        _ctx_2048t = _ctx_2048t * jax.lax.rsqrt(jnp.mean(jnp.square(_ctx_2048t)) + 1e-12) * 0.953939
        ctx_2048 = 0.000189249 + 0.0999589 * (_ctx_2048t + 0.3 * jax.random.normal(jax.random.fold_in(_rk, 611), (8, 256, 512), jnp.float32))
        return (x, ctx_2048)
    x, ctx_2048 = _rec_inputs()

    def _L0_xattn_setup():
        import jax, jax.numpy as jnp
        import numpy as np
        B, L, E, H = (4, 128, 512, 32)
        S = E // H
        EXTRA_MAA, EXTRA_DECAY = (32, 64)
        EPS = 1e-05

        def _ln(x, w, b):
            m = jnp.mean(x, axis=-1, keepdims=True)
            v = jnp.mean((x - m) ** 2, axis=-1, keepdims=True)
            return (x - m) * jax.lax.rsqrt(v + EPS) * w + b

        def _token_shift(xn, prev_row):
            first = (prev_row - xn[:, 0])[:, None]
            rest = xn[:, :-1] - xn[:, 1:]
            return jnp.concatenate([first, rest], axis=1)
        key = jax.random.key(seed)
        ks = jax.random.split(key, 24)
        rn = lambda k, shp, s=1.0: jax.random.normal(k, shp, dtype=jnp.float32) * s
        return dict(x=rn(ks[0], (B, L, E)), state=rn(ks[1], (B, 2 + S, E), 0.1), ln1_w=jnp.ones((E,), jnp.float32), ln1_b=jnp.zeros((E,), jnp.float32), ln2_w=jnp.ones((E,), jnp.float32), ln2_b=jnp.zeros((E,), jnp.float32), maa_x=rn(ks[2], (E,), 0.02), maa_w1=rn(ks[3], (E, 5 * EXTRA_MAA), 0.02), maa_w2=rn(ks[4], (5, EXTRA_MAA, E), 0.02), maa_stack=rn(ks[5], (5, E), 0.02), time_decay=rn(ks[6], (E,), 0.5), decay_w1=rn(ks[7], (E, EXTRA_DECAY), 0.02), decay_w2=rn(ks[8], (EXTRA_DECAY, E), 0.02), faaaa=rn(ks[9], (H, S), 0.1), Wr=rn(ks[10], (E, E), 0.02), Wk=rn(ks[11], (E, E), 0.02), Wv=rn(ks[12], (E, E), 0.02), Wg=rn(ks[13], (E, E), 0.02), Wo=rn(ks[14], (E, E), 0.02), gn_w=jnp.ones((E,), jnp.float32), gn_b=jnp.zeros((E,), jnp.float32), ffn_maa_k=rn(ks[15], (E,), 0.02), ffn_maa_r=rn(ks[16], (E,), 0.02), ffn_Wk=rn(ks[17], (E, E), 0.02), ffn_Wr=rn(ks[18], (E, E), 0.02), ffn_Wv=rn(ks[19], (E, E), 0.02), i=0)
    _L0_xattn_all = _L0_xattn_setup()
    _L0_xattn_in = {k: v for k, v in _L0_xattn_all.items() if k in ('ln1_w', 'ln1_b', 'ln2_w', 'ln2_b', 'maa_x', 'maa_w1', 'maa_w2', 'maa_stack', 'time_decay', 'decay_w1', 'decay_w2', 'faaaa', 'Wr', 'Wk', 'Wv', 'Wg', 'Wo', 'gn_w', 'gn_b', 'ffn_maa_k', 'ffn_maa_r', 'ffn_Wk', 'ffn_Wr', 'ffn_Wv')}
    del _L0_xattn_all
    return {'x': x, 'ctx_2048': ctx_2048, 'L0_xattn_ln1_w': _L0_xattn_in['ln1_w'], 'L0_xattn_ln1_b': _L0_xattn_in['ln1_b'], 'L0_xattn_ln2_w': _L0_xattn_in['ln2_w'], 'L0_xattn_ln2_b': _L0_xattn_in['ln2_b'], 'L0_xattn_maa_x': _L0_xattn_in['maa_x'], 'L0_xattn_maa_w1': _L0_xattn_in['maa_w1'], 'L0_xattn_maa_w2': _L0_xattn_in['maa_w2'], 'L0_xattn_maa_stack': _L0_xattn_in['maa_stack'], 'L0_xattn_time_decay': _L0_xattn_in['time_decay'], 'L0_xattn_decay_w1': _L0_xattn_in['decay_w1'], 'L0_xattn_decay_w2': _L0_xattn_in['decay_w2'], 'L0_xattn_faaaa': _L0_xattn_in['faaaa'], 'L0_xattn_Wr': _L0_xattn_in['Wr'], 'L0_xattn_Wk': _L0_xattn_in['Wk'], 'L0_xattn_Wv': _L0_xattn_in['Wv'], 'L0_xattn_Wg': _L0_xattn_in['Wg'], 'L0_xattn_Wo': _L0_xattn_in['Wo'], 'L0_xattn_gn_w': _L0_xattn_in['gn_w'], 'L0_xattn_gn_b': _L0_xattn_in['gn_b'], 'L0_xattn_ffn_maa_k': _L0_xattn_in['ffn_maa_k'], 'L0_xattn_ffn_maa_r': _L0_xattn_in['ffn_maa_r'], 'L0_xattn_ffn_Wk': _L0_xattn_in['ffn_Wk'], 'L0_xattn_ffn_Wr': _L0_xattn_in['ffn_Wr'], 'L0_xattn_ffn_Wv': _L0_xattn_in['ffn_Wv']}

def reference(x, ctx_2048, L0_xattn_ln1_w, L0_xattn_ln1_b, L0_xattn_ln2_w, L0_xattn_ln2_b, L0_xattn_maa_x, L0_xattn_maa_w1, L0_xattn_maa_w2, L0_xattn_maa_stack, L0_xattn_time_decay, L0_xattn_decay_w1, L0_xattn_decay_w2, L0_xattn_faaaa, L0_xattn_Wr, L0_xattn_Wk, L0_xattn_Wv, L0_xattn_Wg, L0_xattn_Wo, L0_xattn_gn_w, L0_xattn_gn_b, L0_xattn_ffn_maa_k, L0_xattn_ffn_maa_r, L0_xattn_ffn_Wk, L0_xattn_ffn_Wr, L0_xattn_ffn_Wv):
    import jax
    import jax.numpy as jnp

    def _L0_xattn_ref(x, state, ln1_w, ln1_b, ln2_w, ln2_b, maa_x, maa_w1, maa_w2, maa_stack, time_decay, decay_w1, decay_w2, faaaa, Wr, Wk, Wv, Wg, Wo, gn_w, gn_b, ffn_maa_k, ffn_maa_r, ffn_Wk, ffn_Wr, ffn_Wv, i):
        import jax, jax.numpy as jnp
        import numpy as np
        B, L, E, H = (4, 128, 512, 32)
        S = E // H
        EXTRA_MAA, EXTRA_DECAY = (32, 64)
        EPS = 1e-05

        def _ln(x, w, b):
            m = jnp.mean(x, axis=-1, keepdims=True)
            v = jnp.mean((x - m) ** 2, axis=-1, keepdims=True)
            return (x - m) * jax.lax.rsqrt(v + EPS) * w + b

        def _token_shift(xn, prev_row):
            first = (prev_row - xn[:, 0])[:, None]
            rest = xn[:, :-1] - xn[:, 1:]
            return jnp.concatenate([first, rest], axis=1)
        b, l = (x.shape[0], x.shape[1])
        i0 = (2 + S) * i + 0
        i1 = (2 + S) * i + 1
        xn = _ln(x, ln1_w, ln1_b)
        sx = _token_shift(xn, state[:, i1])
        xxx = jnp.tanh((xn + sx * maa_x) @ maa_w1).reshape(b, l, 5, 1, EXTRA_MAA)
        xxx = jnp.matmul(xxx, maa_w2).reshape(b, l, 5, E)
        x5 = xn[:, :, None] + sx[:, :, None] * (maa_stack + xxx)
        w = jnp.exp(-jnp.exp(time_decay + jnp.tanh(x5[:, :, 1] @ decay_w1) @ decay_w2))
        w = w.reshape(b, l, H, S)
        r = (x5[:, :, 3] @ Wr.T).reshape(b, l, H, S)
        k = (x5[:, :, 0] @ Wk.T).reshape(b, l, H, S)
        v = (x5[:, :, 2] @ Wv.T).reshape(b, l, H, S)
        g = jax.nn.silu(x5[:, :, 4] @ Wg.T)
        s0 = state[:, (2 + S) * i + 2:(2 + S) * (i + 1)].reshape(b, H, S, S)
        u = faaaa[None, :, :, None]

        def step(s, rkvw):
            r_t, k_t, v_t, w_t = rkvw
            a = k_t[:, :, :, None] * v_t[:, :, None, :]
            out = jnp.einsum('bhk,bhkd->bhd', r_t, u * a + s)
            return (a + w_t[:, :, :, None] * s, out)
        xs = tuple((jnp.moveaxis(t, 1, 0) for t in (r, k, v, w)))
        _, outs = jax.lax.scan(step, s0, xs)
        att = jnp.moveaxis(outs, 0, 1).reshape(b, l, E)
        a4 = att.reshape(b, l, H, S)
        m = jnp.mean(a4, axis=-1, keepdims=True)
        var = jnp.mean((a4 - m) ** 2, axis=-1, keepdims=True)
        att = ((a4 - m) * jax.lax.rsqrt(var + EPS)).reshape(b, l, E) * gn_w + gn_b
        x = x + att * g @ Wo.T
        xn2 = _ln(x, ln2_w, ln2_b)
        sx2 = _token_shift(xn2, state[:, i0])
        xk = xn2 + sx2 * ffn_maa_k
        xr = xn2 + sx2 * ffn_maa_r
        rr = jax.nn.sigmoid(xr @ ffn_Wr.T)
        kk = jnp.square(jax.nn.relu(xk @ ffn_Wk.T))
        x = x + rr * (kk @ ffn_Wv.T)
        return x
    x = _L0_xattn_ref(x, ctx_2048, L0_xattn_ln1_w, L0_xattn_ln1_b, L0_xattn_ln2_w, L0_xattn_ln2_b, L0_xattn_maa_x, L0_xattn_maa_w1, L0_xattn_maa_w2, L0_xattn_maa_stack, L0_xattn_time_decay, L0_xattn_decay_w1, L0_xattn_decay_w2, L0_xattn_faaaa, L0_xattn_Wr, L0_xattn_Wk, L0_xattn_Wv, L0_xattn_Wg, L0_xattn_Wo, L0_xattn_gn_w, L0_xattn_gn_b, L0_xattn_ffn_maa_k, L0_xattn_ffn_maa_r, L0_xattn_ffn_Wk, L0_xattn_ffn_Wr, L0_xattn_ffn_Wv, 0)
    return x

_drawn_inputs = setup_inputs


def setup_inputs(seed=0):
    import zlib

    import numpy as np

    out = dict(_drawn_inputs(seed))
    spreads = {'L0_xattn_ln1_w': (1.0, 0.2),
     'L0_xattn_ln1_b': (0.0, 0.1),
     'L0_xattn_ln2_w': (1.0, 0.6),
     'L0_xattn_ln2_b': (0.0, 0.8),
     'L0_xattn_gn_w': (1.0, 0.6),
     'L0_xattn_gn_b': (0.0, 0.676)}
    factors = {'ctx_2048': 25.957,
     'L0_xattn_maa_x': 8.0,
     'L0_xattn_maa_w1': 2.875,
     'L0_xattn_maa_w2': 2.9,
     'L0_xattn_maa_stack': 6.325,
     'L0_xattn_decay_w1': 8.0,
     'L0_xattn_decay_w2': 8.0,
     'L0_xattn_faaaa': 2.976,
     'L0_xattn_ffn_maa_k': 8.0,
     'L0_xattn_ffn_maa_r': 8.0,
     'L0_xattn_ffn_Wr': 4.128}
    for name, (base, spread) in spreads.items():
        noise = np.random.default_rng([zlib.crc32(name.encode()), seed]).standard_normal(out[name].shape)
        drawn = base * np.exp(spread * noise) if base else spread * noise
        out[name] = jnp.asarray(drawn.astype(out[name].dtype))
    for name, factor in factors.items():
        out[name] = (out[name] * factor).astype(out[name].dtype)
    return out
```

```python
from contextlib import ExitStack

import numpy as np

import concourse.bass as bass
from concourse import mybir

ALU = mybir.AluOpType
ACT = mybir.ActivationFunctionType
AX = mybir.AxisListType
F32 = mybir.dt.float32

B, L, E, H = 8, 256, 512, 32
S = E // H
P = 128
C = E // P
T = L // P
HP = P // S
LORA, NMIX, DEC = 32, 5, 64
EPS = 1e-5
PAIRS = B // 2 - 1

(LN1_W, LN1_B, LN2_W, LN2_B, MAA_X, MAA_STACK, TIME_DECAY, FAAAA, GN_W, GN_B, FFN_MAA_K, FFN_MAA_R,
 PREV_ATT, PREV_FFN, NCOLS) = (0, 1, 2, 3, 4, 5, 10, 11, 12, 13, 14, 15, 16, 16 + B, 16 + 2 * B)

MIXES = (1, 0, 2, 3, 4)

DIRECT = ((0, 0, 4), (1, 0, 4), (2, 0, 4), (4, 0, 2), (4, 2, 2), (8, 0, 1), (8, 1, 1), (8, 2, 1), (8, 3, 1))
ND = len(DIRECT)
STATE = ((16, 0, 1), (16, 1, 1), (16, 2, 1), (16, 3, 1), (32, 0, 2), (32, 2, 2), (64, 0, 4), (128, 0, 4))
NS = len(STATE)
LEVELS = (16, 32, 64, 128)

SCHEDULE = (
    "f_stats", "b_direct0", "b_direct1", "f_norm", "b_direct2", "b_direct3", "f_lora", "b_direct4",
    "f_mix0", "b_direct5", "f_mix1", "f_dec1", "b_direct6", "f_dec2", "f_mix2", "b_direct7", "f_k", "b_direct8",
    "b_vtok", "b_ktok16", "b_kv0", "b_kv1", "b_apply0", "b_kv2", "b_apply1", "b_kv3", "b_apply2", "b_apply3",
    "f_mix3", "f_v",
    "b_ktok32", "b_kv4", "b_kv5", "b_apply4", "b_apply5", "b_ktok64", "f_mix4", "b_kv6", "b_apply6", "b_ktok128",
    "b_kv7", "b_apply7", "b_s0", "b_att", "f_r", "b_gn", "b_wo", "f_g", "b_norm2", "b_mix2", "b_ffn", "b_out",
)


def spread(ap, axis, n):
    shape = list(ap.shape)
    shape[axis] = n
    return ap.broadcast_to(shape)


def wkv_kernel(nc, x, cols, s0, w1, w2a, w2b, dw1, dw2, wk, wv, wr, wg, wo, fk, fr, fv, ident, headmask, tokmask, out):
    with ExitStack() as ctx:
        def sb(name, shape):
            return ctx.enter_context(nc.sbuf_tensor(name, shape, F32))

        def sem(name):
            return ctx.enter_context(nc.semaphore(name))

        cols_s = sb("cols_s", [P, C, NCOLS])
        s0_s = sb("s0_s", [P, B, C, S])
        ident_s = sb("ident_s", [P, P])
        hm_s = sb("hm_s", [P, P])
        tm_s = sb("tm_s", [P, 7])
        u_s = sb("u_s", [P, C, P])
        w1_s = sb("w1_s", [P, C, NMIX * LORA])
        w2a_s = sb("w2a_s", [P, E])
        w2b_s = sb("w2b_s", [LORA, E])
        dw1_s = sb("dw1_s", [P, C, DEC])
        dw2_s = sb("dw2_s", [DEC, E])
        big = {n: sb(n + "_s", [P, C, E]) for n in ("wk", "wv", "wr", "wg", "wo", "fk", "fr", "fv")}
        pause = sb("pause", [P, 1])
        eps_s = sb("eps_s", [P, T * H])
        half_s = sb("half_s", [P, T * H])

        xt = sb("xt", [P, 2, T, E])
        st1 = sb("st1", [P, T, 6])
        mv1 = sb("mv1", [P, T, 2])
        ve1 = sb("ve1", [P, T])
        rs1 = sb("rs1", [P, T])
        xhat = sb("xhat", [P, T, E])
        xnT = sb("xnT", [P, C, L + 1])
        sx = sb("sx", [P, C, L])
        xmix = sb("xmix", [P, 2, C, L])
        thA = sb("thA", [P, L])
        thB = sb("thB", [LORA, L])
        dech = sb("dech", [DEC, L])
        rT, kT, vT, wT, gT = (sb(n, [P, 2, C * L]) for n in ("rT", "kT", "vT", "wT", "gT"))

        pp = sb("pp", [P, 2, 1024])
        qs = sb("qs", [P, 512])
        acc = sb("acc", [P, C * L])
        tot = sb("tot", [P, 1024])
        vtok = sb("vtok", [P, T, E])
        kexp = sb("kexp", [P, 4, T, E])
        sring = pp
        s0bd = sb("s0bd", [P, C, HP, S])
        gsum = sb("gsum", [P, T * H])
        gvar = sb("gvar", [P, T * H])
        gve = sb("gve", [P, T * H])
        grs = sb("grs", [P, T * H])
        cen = sb("cen", [P, T, E])
        x1 = sb("x1", [P, T, E])
        qb = x1[:, :, :].rearrange("p t e -> p (t e)")
        st2 = sb("st2", [P, T, 6])
        mv2 = sb("mv2", [P, T, 2])
        ve2 = sb("ve2", [P, T])
        rs2 = sb("rs2", [P, T])
        xn2T = sb("xn2T", [P, C, L + 1])
        xhat2 = cen
        xk = kexp[:, 0, :, :].rearrange("p t e -> p (t e)").rearrange("p (c l) -> p c l", c=C)
        xr = kexp[:, 1, :, :].rearrange("p t e -> p (t e)").rearrange("p (c l) -> p c l", c=C)
        kk = xk
        rr = kexp[:, 2, :, :]
        sq = rr
        yb = kexp[:, 3, :, :].rearrange("p t e -> p (t e)").rearrange("p (c l) -> p c l", c=C)
        sx2 = yb
        outt = kexp[:, 3, :, :]

        FA, FB, BA, BB = (ctx.enter_context(nc.psum_tensor(n, [P, 1024], F32)) for n in ("FA", "FB", "BA", "BB"))

        c_loaded = sem("c_loaded")
        w_loaded = {n: sem(n + "_loaded") for n in
                    ("w1", "w2", "dw", "wk", "wv", "wr", "wg", "wo", "fk", "fr", "fv")}
        x_loaded = [sem("x_loaded0"), sem("x_loaded1")]
        half_ready = sem("half_ready")
        u_ready = sem("u_ready")
        names = (
            "st1_ready mv1_ready ve1_ready rs1_ready xhat_ready xhatT_ready xnT_ready sx_ready xin_ready lora_ready "
            "th_ready m2_ready mixm_ready mix_ready dech_ready dec1_ready dec2_ready wexp_ready w_ready "
            "k_ready v_ready r_ready gate_ready g_ready projk_ready projv_ready projr_ready projg_ready "
            "p_ready score_ready q_ready qs_ready acc_ready step_ready vtokT_ready vtok_ready ktokT_ready ktok_ready "
            "kv_ready s_ready rstep_ready applied s0bd_ready o_ready att_ready attT_ready gsum_ready cen_ready sq_ready gvar_ready "
            "gve_ready grs_ready nrm_ready nrmT_ready y1_ready y_ready wo_ready x1_ready st2_ready mv2_ready ve2_ready "
            "rs2_ready xhat2_ready xhat2T_ready xn2T_ready sx2_ready xk_ready xr_ready fr_ready rr_ready fk_ready "
            "relu_ready kk_ready fv_ready mul_ready out_ready stored").split()
        s_ = {n: sem(n) for n in names}

        def blocks(ap, m):
            return ap.rearrange("p (n two m) -> p n two m", two=2, m=m)

        def totals(m):
            at = sum(C * L // q for q in (2, 4, 8, 16, 32, 64, 128) if q < m)
            return tot[:, at:at + C * L // m]

        def pslot(b, par, i):
            return pp[:, (i + par) % 2, :]

        block = ctx.enter_context(nc.Block())

        def walk(eng, steps):
            def run(front, back):
                for name in SCHEDULE:
                    which = front if name[0] == "f" else back
                    if name in steps and which is not None:
                        steps[name](*which)
            run((0, 0, 0), None)
            run((1, 1, 0), (0, 0, 0))
            with eng.Fori(0, PAIRS) as j:
                run((2 * j + 2, 0, j + 1), (2 * j + 1, 1, j))
                run((2 * j + 3, 1, j + 1), (2 * j + 2, 0, j + 1))
            run(None, (B - 1, 1, B // 2 - 1))

        def first(b):
            return isinstance(b, int) and b == 0

        @block.sync
        def _(sp):
            def load_x(b, par):
                sp.dma_start(xt[:, par], x[b].rearrange("(t p) e -> p t e", p=P)).then_inc(x_loaded[par], 16)

            load_x(0, 0)
            for dst, src in ((cols_s, cols), (ident_s, ident), (hm_s, headmask), (tm_s, tokmask), (s0_s, s0)):
                sp.dma_start(dst[:], src).then_inc(c_loaded, 16)
            sp.dma_start(w1_s[:], w1).then_inc(w_loaded["w1"], 16)
            sp.dma_start(w2a_s[:], w2a).then_inc(w_loaded["w2"], 16)
            sp.dma_start(w2b_s[:], w2b).then_inc(w_loaded["w2"], 16)
            sp.dma_start(dw1_s[:], dw1).then_inc(w_loaded["dw"], 16)
            sp.dma_start(dw2_s[:], dw2).then_inc(w_loaded["dw"], 16)
            load_x(1, 1)
            for n, src in (("wk", wk), ("wv", wv), ("wr", wr), ("wg", wg), ("wo", wo), ("fr", fr), ("fk", fk),
                           ("fv", fv)):
                sp.dma_start(big[n][:], src).then_inc(w_loaded[n], 16)

            def store(b):
                sp.wait_ge(s_["out_ready"], b + 1)
                sp.dma_start(out[b].rearrange("(t p) e -> p t e", p=P), outt).then_inc(s_["stored"], 16)

            def reload(b, par):
                sp.wait_ge(s_["x1_ready"], b - 1)
                load_x(b, par)

            reload(2, 0)
            store(0)
            with sp.Fori(0, PAIRS - 1) as j:
                reload(2 * j + 3, 1)
                store(2 * j + 1)
                reload(2 * j + 4, 0)
                store(2 * j + 2)
            reload(B - 1, 1)
            store(B - 3)
            store(B - 2)
            store(B - 1)
            sp.wait_ge(s_["stored"], 16 * B)

        @block.gpsimd
        def _(pool):
            nc.gpsimd.memset(half_s[:], -0.5).then_inc(half_ready, 1)
            nc.gpsimd.memset(eps_s[:], EPS).then_inc(half_ready, 1)
            pool.wait_ge(half_ready, 2)
            pool.wait_ge(c_loaded, 16 * 5)
            for c in range(C):
                nc.gpsimd.tensor_tensor(u_s[:, c, :], hm_s[:], spread(cols_s[:, c, FAAAA:FAAAA + 1], 1, P),
                                        ALU.mult).then_inc(u_ready, 1)

            def inverse_root(mv_ready, mv, ve, ve_ready, rs, rs_ready, b):
                pool.wait_ge(mv_ready, b + 1)
                nc.gpsimd.tensor_tensor(ve[:], mv, eps_s[:, 0:T], ALU.add).then_inc(ve_ready, 1)
                pool.wait_ge(ve_ready, b + 1)
                nc.gpsimd.tensor_tensor(rs[:], ve[:], half_s[:, 0:T], ALU.pow).then_inc(rs_ready, 1)

            def f_stats(b, par, n):
                inverse_root(s_["mv1_ready"], mv1[:, :, 1], ve1, s_["ve1_ready"], rs1, s_["rs1_ready"], b)

            def f_norm(b, par, n):
                pool.wait_ge(s_["xnT_ready"], b + 1)
                if not first(b):
                    pool.wait_ge(s_["mixm_ready"], NMIX * b)
                nc.gpsimd.tensor_tensor(sx[:], xnT[:, :, 0:L], xnT[:, :, 1:L + 1],
                                        ALU.subtract).then_inc(s_["sx_ready"], 1)

            def f_mix(j):
                def run(b, par, n):
                    pool.wait_ge(s_["mixm_ready"], NMIX * b + j + 1)
                    slot = xmix[:, (j + 1) % 2]
                    nc.gpsimd.tensor_tensor(slot, slot, xnT[:, :, 1:L + 1], ALU.add).then_inc(s_["mix_ready"], 1)
                return run

            def b_direct(i):
                m, c0, nc_ = DIRECT[i]

                def run(b, par, n):
                    r, k = rT[:, par, c0 * L:(c0 + nc_) * L], kT[:, par, c0 * L:(c0 + nc_) * L]
                    if m == 0:
                        pool.wait_ge(s_["r_ready"], b + 1)
                        pool.wait_ge(s_["k_ready"], b + 1)
                        if not first(b):
                            pool.wait_ge(s_["o_ready"], b)
                    elif m > 1 and c0 == 0:
                        pool.wait_ge(s_["step_ready"], 7 * b + {2: 1, 4: 2, 8: 3}[m])
                    if i >= 2:
                        pool.wait_ge(s_["score_ready"], ND * b + i - 1)
                    slot = pslot(b, par, i)
                    if m == 0:
                        ins = nc.gpsimd.tensor_tensor(slot, r, k, ALU.mult)
                    elif m == 1:
                        ins = nc.gpsimd.tensor_tensor(slot[:, 0:C * L // 2], blocks(r, 1)[:, :, 1, 0],
                                                      blocks(k, 1)[:, :, 0, 0], ALU.mult)
                    else:
                        ins = nc.gpsimd.tensor_tensor(
                            slot.rearrange("p (n i j) -> p n i j", i=m, j=m),
                            spread(blocks(r, m)[:, :, 1, :].unsqueeze(3), 3, m),
                            spread(blocks(k, m)[:, :, 0, :].unsqueeze(2), 2, m), ALU.mult)
                    ins.then_inc(s_["p_ready"], 1)
                return run

            def b_vtok(b, par, n):
                if not first(b):
                    pool.wait_ge(s_["o_ready"], b)
                nc.gpsimd.tensor_tensor(
                    s0bd[:], spread(s0_s[:, b, :, :].unsqueeze(2), 2, HP),
                    spread(hm_s[:, :].rearrange("p (h s) -> p h s", h=HP).unsqueeze(1), 1, C),
                    ALU.mult).then_inc(s_["s0bd_ready"], 1)

            def b_gn(b, par, n):
                pool.wait_ge(s_["gvar_ready"], b + 1)
                nc.gpsimd.tensor_tensor(gve[:], gvar[:], eps_s[:], ALU.add).then_inc(s_["gve_ready"], 1)
                pool.wait_ge(s_["gve_ready"], b + 1)
                nc.gpsimd.tensor_tensor(grs[:], gve[:], half_s[:], ALU.pow).then_inc(s_["grs_ready"], 1)
                pool.wait_ge(s_["grs_ready"], b + 1)
                c3 = cen[:, :, :].rearrange("p t e -> p (t e)").rearrange("p (h s) -> p h s", s=S)
                nc.gpsimd.tensor_tensor(c3, c3, spread(grs[:, :].unsqueeze(2), 2, S),
                                        ALU.mult).then_inc(s_["nrm_ready"], 1)

            def b_wo(b, par, n):
                inverse_root(s_["mv2_ready"], mv2[:, :, 1], ve2, s_["ve2_ready"], rs2, s_["rs2_ready"], b)

            def b_norm2(b, par, n):
                pool.wait_ge(s_["xn2T_ready"], b + 1)
                nc.gpsimd.tensor_tensor(sx2, xn2T[:, :, 0:L], xn2T[:, :, 1:L + 1],
                                        ALU.subtract).then_inc(s_["sx2_ready"], 1)

            steps = dict(f_stats=f_stats, f_norm=f_norm, b_vtok=b_vtok, b_gn=b_gn, b_wo=b_wo, b_norm2=b_norm2)
            steps.update({f"f_mix{j}": f_mix(j) for j in range(NMIX)})
            steps.update({f"b_direct{i}": b_direct(i) for i in range(ND)})
            walk(pool, steps)

        @block.tensor
        def _(pe):
            def transpose_tokens(dst, src):
                for t in range(T):
                    for c in range(C):
                        ins = nc.tensor.transpose(dst[:, t * E + c * P:t * E + (c + 1) * P],
                                                  src[:, c * L + t * P:c * L + (t + 1) * P], ident_s[:])
                return ins

            def transpose_channels(dst, src):
                for c in range(C):
                    for t in range(T):
                        ins = nc.tensor.transpose(dst[:, c * L + t * P:c * L + (t + 1) * P],
                                                  src[:, t, c * P:(c + 1) * P], ident_s[:])
                return ins

            def project(dst, weight, src):
                for c in range(C):
                    for q in range(C):
                        ins = nc.tensor.matmul(dst[:, c * L:(c + 1) * L], weight[:, q, c * P:(c + 1) * P],
                                               src[:, q, :], start=(q == 0), stop=(q == C - 1))
                return ins

            def project_tokens(dst, weight, src):
                for t in range(T):
                    for q in range(C):
                        ins = nc.tensor.matmul(dst[:, t * E:(t + 1) * E], src[:, q, t * P:(t + 1) * P],
                                               weight[:, q, :], start=(q == 0), stop=(q == C - 1))
                return ins

            def loaded(name, n=16):
                pe.wait_ge(w_loaded[name], n)

            def f_norm(b, par, n):
                if first(b):
                    pe.wait_ge(c_loaded, 16 * 5)
                pe.wait_ge(s_["xhat_ready"], b + 1)
                if not first(b):
                    pe.wait_ge(s_["mixm_ready"], NMIX * b)
                transpose_channels(FA, xhat).then_inc(s_["xhatT_ready"], 1)

            def f_lora(b, par, n):
                loaded("w1")
                pe.wait_ge(s_["xin_ready"], b + 1)
                if not first(b):
                    pe.wait_ge(s_["g_ready"], b)
                    pe.wait_ge(s_["gate_ready"], b)
                for q in range(C):
                    nc.tensor.matmul(FB[:, 0:L], w1_s[:, q, 0:P], xmix[:, 0, q, :], start=(q == 0), stop=(q == C - 1))
                for q in range(C):
                    ins = nc.tensor.matmul(FB[0:LORA, 512:512 + L], w1_s[:, q, P:P + LORA], xmix[:, 0, q, :],
                                           start=(q == 0), stop=(q == C - 1))
                ins.then_inc(s_["lora_ready"], 1)

            def f_mix(j):
                i = MIXES[j]

                def run(b, par, n):
                    if j == 0:
                        loaded("w2", 32)
                        pe.wait_ge(s_["th_ready"], 2 * b + 2)
                    else:
                        pe.wait_ge(s_["mixm_ready"], NMIX * b + j)
                    for c in range(C):
                        if i < 4:
                            lhs, rhs = w2a_s[32 * i:32 * i + 32, c * P:(c + 1) * P], thA[32 * i:32 * i + 32, :]
                        else:
                            lhs, rhs = w2b_s[:, c * P:(c + 1) * P], thB[:, :]
                        ins = nc.tensor.matmul(FA[:, c * L:(c + 1) * L], lhs, rhs, start=True, stop=True)
                    ins.then_inc(s_["m2_ready"], 1)
                return run

            def f_dec1(b, par, n):
                loaded("dw", 32)
                pe.wait_ge(s_["mix_ready"], NMIX * b + 1)
                pe.wait_ge(s_["th_ready"], 2 * b + 2)
                for q in range(C):
                    ins = nc.tensor.matmul(FB[0:DEC, 0:L], dw1_s[:, q, :], xmix[:, 1, q, :],
                                           start=(q == 0), stop=(q == C - 1))
                ins.then_inc(s_["dec1_ready"], 1)

            def f_dec2(b, par, n):
                pe.wait_ge(s_["dech_ready"], b + 1)
                for c in range(C):
                    ins = nc.tensor.matmul(FB[:, c * L:(c + 1) * L], dw2_s[:, c * P:(c + 1) * P], dech[:],
                                           start=True, stop=True)
                ins.then_inc(s_["dec2_ready"], 1)

            def f_proj(read, j, weight, done):
                def run(b, par, n):
                    loaded(weight)
                    pe.wait_ge(s_["mix_ready"], NMIX * b + j + 1)
                    pe.wait_ge(s_[read], b + 1)
                    project(FB, big[weight], xmix[:, (j + 1) % 2]).then_inc(s_[done], 1)
                return run

            def b_direct(i):
                m, c0, nc_ = DIRECT[i]
                dst = BA if i % 2 == 0 else BB

                def run(b, par, n):
                    pe.wait_ge(s_["p_ready"], ND * b + i + 1)
                    if i == 0:
                        pe.wait_ge(u_ready, C)
                        pe.wait_ge(s_["out_ready"], b)
                    elif i == 1:
                        if not first(b):
                            pe.wait_ge(s_["relu_ready"], b)
                    else:
                        pe.wait_ge(s_["q_ready"], ND * b + i - 1)
                    slot = pslot(b, par, i)
                    if m == 0:
                        for c in range(C):
                            ins = nc.tensor.matmul(dst[:, c * L:(c + 1) * L], u_s[:, c, :], slot[:, c * L:(c + 1) * L],
                                                   start=True, stop=True)
                    else:
                        for h in range(1 if m == 1 else 2):
                            ins = nc.tensor.matmul(dst[:, h * 512:(h + 1) * 512], hm_s[:],
                                                   slot[:, h * 512:(h + 1) * 512], start=True, stop=True)
                    ins.then_inc(s_["score_ready"], 1)
                return run

            def b_vtok(b, par, n):
                pe.wait_ge(s_["v_ready"], b + 1)
                pe.wait_ge(s_["q_ready"], ND * b + ND)
                transpose_tokens(BA, vT[:, par, :]).then_inc(s_["vtokT_ready"], 1)

            def b_ktok(l):
                m = LEVELS[l]

                def run(b, par, n):
                    pe.wait_ge(s_["step_ready"], 7 * b + (4, 5, 6, 7)[l])
                    if l == 0:
                        pe.wait_ge(s_["vtok_ready"], b + 1)
                    else:
                        q = [i for i, st in enumerate(STATE) if st[0] == m][0]
                        pe.wait_ge(s_["s_ready"], NS * b + q)
                    src = kT[:, par, :]
                    if m < P:
                        ins = transpose_tokens(BA, src)
                    else:
                        for c in range(C):
                            ins = nc.tensor.transpose(BA[:, c * P:(c + 1) * P], src[:, c * L:c * L + P], ident_s[:])
                    ins.then_inc(s_["ktokT_ready"], 1)
                return run

            def pieces(q):
                m, c0, nc_ = STATE[q]
                nb = L // (2 * m)
                return [(j, c0 + j // nb, j % nb) for j in range(nc_ * nb)]

            def b_kv(q):
                m = STATE[q][0]

                def run(b, par, n):
                    pe.wait_ge(s_["ktok_ready"], 4 * b + LEVELS.index(m) + 1)
                    if q > 0 and STATE[q - 1][0] == m:
                        pe.wait_ge(s_["s_ready"], NS * b + q)
                    for j, c, i in pieces(q):
                        per = max(P // (2 * m), 1)
                        ins = nc.tensor.matmul(BA[:, j * P:(j + 1) * P], kexp[:, i % per, i // per, c * P:(c + 1) * P],
                                               vtok[:, i // per, c * P:(c + 1) * P], start=True, stop=True)
                    ins.then_inc(s_["kv_ready"], 1)
                return run

            def b_apply(q):
                m = STATE[q][0]

                def run(b, par, n):
                    if q == 0:
                        pe.wait_ge(s_["step_ready"], 7 * b + 4)
                    if q > 0 and STATE[q - 1][0] != m:
                        pe.wait_ge(s_["rstep_ready"], 4 * b + LEVELS.index(m))
                    pe.wait_ge(s_["s_ready"], NS * b + q + 1)
                    for j, c, i in pieces(q):
                        t0 = 2 * m * i + m
                        ins = nc.tensor.matmul(BB[:, c * L + t0:c * L + t0 + m], sring[:, q % 2, j * P:(j + 1) * P],
                                               rT[:, par, c * L + t0:c * L + t0 + m],
                                               start=(m == LEVELS[0] and c % 2 == 0 and i == 0), stop=False,
                                               skip_group_check=True)
                    ins.then_inc(s_["applied"], 1)
                return run

            def b_s0(b, par, n):
                pe.wait_ge(s_["rstep_ready"], 4 * b + 4)
                pe.wait_ge(s_["s0bd_ready"], b + 1)
                for c in range(C):
                    ins = nc.tensor.matmul(BB[:, c * L:(c + 1) * L],
                                           s0bd[:, c, :, :].rearrange("p h s -> p (h s)"),
                                           rT[:, par, c * L:(c + 1) * L], start=False, stop=True,
                                           skip_group_check=True)
                ins.then_inc(s_["o_ready"], 1)

            def b_att(b, par, n):
                pe.wait_ge(s_["att_ready"], b + 1)
                pe.wait_ge(s_["s_ready"], NS * b + NS)
                transpose_tokens(BA, acc[:, :]).then_inc(s_["attT_ready"], 1)

            def b_gn(b, par, n):
                pe.wait_ge(s_["nrm_ready"], b + 1)
                transpose_channels(BA, cen).then_inc(s_["nrmT_ready"], 1)

            def b_wo(b, par, n):
                loaded("wo")
                pe.wait_ge(s_["y_ready"], b + 1)
                project_tokens(BA, big["wo"], yb).then_inc(s_["wo_ready"], 1)

            def b_norm2(b, par, n):
                pe.wait_ge(s_["xhat2_ready"], b + 1)
                transpose_channels(BA, xhat2).then_inc(s_["xhat2T_ready"], 1)

            def b_ffn(b, par, n):
                loaded("fr")
                pe.wait_ge(s_["xr_ready"], b + 1)
                project_tokens(BA, big["fr"], xr).then_inc(s_["fr_ready"], 1)
                loaded("fk")
                pe.wait_ge(s_["xk_ready"], b + 1)
                project(BB, big["fk"], xk).then_inc(s_["fk_ready"], 1)

            def b_out(b, par, n):
                loaded("fv")
                pe.wait_ge(s_["rr_ready"], b + 1)
                pe.wait_ge(s_["kk_ready"], b + 1)
                project_tokens(BA, big["fv"], kk).then_inc(s_["fv_ready"], 1)

            steps = dict(f_norm=f_norm, f_lora=f_lora, f_dec1=f_dec1, f_dec2=f_dec2,
                         f_k=f_proj("wexp_ready", 1, "wk", "projk_ready"), f_v=f_proj("k_ready", 2, "wv", "projv_ready"),
                         f_r=f_proj("v_ready", 3, "wr", "projr_ready"), f_g=f_proj("r_ready", 4, "wg", "projg_ready"),
                         b_vtok=b_vtok, b_s0=b_s0, b_att=b_att, b_gn=b_gn, b_wo=b_wo, b_norm2=b_norm2,
                         b_ffn=b_ffn, b_out=b_out)
            steps.update({f"f_mix{j}": f_mix(j) for j in range(NMIX)})
            steps.update({f"b_direct{i}": b_direct(i) for i in range(ND)})
            steps.update({f"b_ktok{m}": b_ktok(l) for l, m in enumerate(LEVELS)})
            steps.update({f"b_kv{q}": b_kv(q) for q in range(NS)})
            steps.update({f"b_apply{q}": b_apply(q) for q in range(NS)})
            walk(pe, steps)

        @block.scalar
        def _(act):
            def col(i):
                return lambda c: cols_s[:, c, i:i + 1]

            def f_norm(b, par, n):
                if first(b):
                    act.wait_ge(c_loaded, 16 * 5)
                else:
                    act.wait_ge(s_["mix_ready"], NMIX * b)
                act.wait_ge(s_["xhatT_ready"], b + 1)
                nc.scalar.activation(xnT[:, :, 0:1], cols_s[:, :, bass.ds(PREV_ATT + b, 1)], ACT.Copy)
                for c in range(C):
                    ins = nc.scalar.activation(xnT[:, c, 1:L + 1], FA[:, c * L:(c + 1) * L], ACT.Identity,
                                               bias=col(LN1_B)(c), scale=col(LN1_W)(c))
                ins.then_inc(s_["xnT_ready"], 1)

            def f_lora(b, par, n):
                act.wait_ge(s_["lora_ready"], b + 1)
                if not first(b):
                    act.wait_ge(s_["m2_ready"], NMIX * b)
                nc.scalar.activation(thA[:], FB[:, 0:L], ACT.Tanh).then_inc(s_["th_ready"], 1)
                ins = nc.scalar.activation(thB[:], FB[0:LORA, 512:512 + L], ACT.Tanh)
                ins.then_inc(s_["th_ready"], 1)

            def f_dec1(b, par, n):
                act.wait_ge(s_["dec1_ready"], b + 1)
                nc.scalar.activation(dech[:], FB[0:DEC, 0:L], ACT.Tanh).then_inc(s_["dech_ready"], 1)

            def f_dec2(b, par, n):
                act.wait_ge(s_["dec2_ready"], b + 1)
                if not first(b):
                    act.wait_ge(s_["o_ready"], b - 1)
                for c in range(C):
                    ins = nc.scalar.activation(wT[:, par, c * L:(c + 1) * L], FB[:, c * L:(c + 1) * L], ACT.Exp,
                                               bias=col(TIME_DECAY)(c))
                ins.then_inc(s_["wexp_ready"], 1)
                act.wait_ge(s_["wexp_ready"], b + 1)
                nc.scalar.activation(wT[:, par, :], wT[:, par, :], ACT.Exp, scale=-1.0).then_inc(s_["w_ready"], 1)

            def f_proj(done, dst, ready):
                def run(b, par, n):
                    act.wait_ge(s_[done], b + 1)
                    if not first(b):
                        act.wait_ge(s_["o_ready"], b - 1)
                    nc.scalar.copy(dst[:, par, :], FB[:]).then_inc(s_[ready], 1)
                return run

            def f_g(b, par, n):
                act.wait_ge(s_["projg_ready"], b + 1)
                if not first(b):
                    act.wait_ge(s_["y_ready"], b - 1)
                nc.scalar.activation(gT[:, par, :], FB[:], ACT.Tanh, scale=0.5).then_inc(s_["gate_ready"], 1)

            def b_vtok(b, par, n):
                act.wait_ge(s_["vtokT_ready"], b + 1)
                nc.scalar.copy(vtok[:, :, :].rearrange("p t e -> p (t e)"), BA[:]).then_inc(s_["vtok_ready"], 1)

            def b_ktok(l):
                m = LEVELS[l]

                def run(b, par, n):
                    act.wait_ge(s_["ktokT_ready"], 4 * b + l + 1)
                    if l == 0:
                        if not first(b):
                            act.wait_ge(s_["stored"], 16 * b)
                    else:
                        q = [i for i, st in enumerate(STATE) if st[0] == m][0]
                        act.wait_ge(s_["kv_ready"], NS * b + q)
                    if m < P:
                        at = {16: 0, 32: 4, 64: 6}[m]
                        for i in range(P // (2 * m)):
                            ins = nc.scalar.activation(kexp[:, i, :, :].rearrange("p t e -> p (t e)"), BA[:],
                                                       ACT.Copy, scale=tm_s[:, at + i:at + i + 1])
                    else:
                        ins = nc.scalar.copy(kexp[:, 0, 0, :], BA[:, 0:E])
                    ins.then_inc(s_["ktok_ready"], 1)
                return run

            def b_att(b, par, n):
                act.wait_ge(s_["cen_ready"], b + 1)
                nc.scalar.activation(sq.rearrange("p t e -> p (t e)"),
                                     cen[:, :, :].rearrange("p t e -> p (t e)"), ACT.Square,
                                     scale=S ** -0.5).then_inc(s_["sq_ready"], 1)

            def b_gn(b, par, n):
                act.wait_ge(s_["nrmT_ready"], b + 1)
                for c in range(C):
                    ins = nc.scalar.activation(yb[:, c, :], BA[:, c * L:(c + 1) * L], ACT.Identity,
                                               bias=col(GN_B)(c), scale=col(GN_W)(c))
                ins.then_inc(s_["y1_ready"], 1)

            def b_norm2(b, par, n):
                act.wait_ge(s_["xhat2T_ready"], b + 1)
                nc.scalar.activation(xn2T[:, :, 0:1], cols_s[:, :, bass.ds(PREV_FFN + b, 1)], ACT.Copy)
                for c in range(C):
                    ins = nc.scalar.activation(xn2T[:, c, 1:L + 1], BA[:, c * L:(c + 1) * L], ACT.Identity,
                                               bias=col(LN2_B)(c), scale=col(LN2_W)(c))
                ins.then_inc(s_["xn2T_ready"], 1)

            def b_ffn(b, par, n):
                act.wait_ge(s_["fr_ready"], b + 1)
                nc.scalar.activation(rr.rearrange("p t e -> p (t e)"), BA[:], ACT.Tanh,
                                     scale=0.5).then_inc(s_["rr_ready"], 1)
                act.wait_ge(s_["fk_ready"], b + 1)
                kf = kk.rearrange("p c l -> p (c l)")
                nc.scalar.activation(kf, BB[:], ACT.Relu).then_inc(s_["relu_ready"], 1)
                act.wait_ge(s_["relu_ready"], b + 1)
                nc.scalar.activation(kf, kf, ACT.Square).then_inc(s_["kk_ready"], 1)

            steps = dict(f_norm=f_norm, f_lora=f_lora, f_dec1=f_dec1, f_dec2=f_dec2,
                         f_k=f_proj("projk_ready", kT, "k_ready"), f_v=f_proj("projv_ready", vT, "v_ready"),
                         f_r=f_proj("projr_ready", rT, "r_ready"), f_g=f_g,
                         b_vtok=b_vtok, b_att=b_att, b_gn=b_gn, b_norm2=b_norm2, b_ffn=b_ffn)
            steps.update({f"b_ktok{m}": b_ktok(l) for l, m in enumerate(LEVELS)})
            walk(act, steps)

        @block.vector
        def _(dve):
            def stats(src, st, st_ready, mv, mv_ready, b):
                for t in range(T):
                    ins = nc.vector.bn_stats(st[:, t, :], src[:, t, :])
                ins.then_inc(st_ready, 1)
                dve.wait_ge(st_ready, b + 1)
                nc.vector.memset(pause[:], 0.0)
                for t in range(T):
                    ins = nc.vector.bn_aggr(mv[:, t, :], st[:, t, :])
                ins.then_inc(mv_ready, 1)

            def norm(dst, src, mv, rs):
                for t in range(T):
                    ins = nc.vector.tensor_scalar(dst[:, t, :], src[:, t, :], mv[:, t, 0:1], rs[:, t:t + 1],
                                                  ALU.subtract, ALU.mult)
                return ins

            def f_stats(b, par, n):
                dve.wait_ge(x_loaded[par], 16 * n + 16)
                stats(xt[:, par], st1, s_["st1_ready"], mv1, s_["mv1_ready"], b)

            def f_norm(b, par, n):
                dve.wait_ge(s_["rs1_ready"], b + 1)
                if not first(b):
                    dve.wait_ge(s_["xhatT_ready"], b)
                norm(xhat, xt[:, par], mv1, rs1).then_inc(s_["xhat_ready"], 1)

            def f_lora(b, par, n):
                dve.wait_ge(s_["sx_ready"], b + 1)
                if not first(b):
                    dve.wait_ge(s_["projr_ready"], b)
                for c in range(C):
                    ins = nc.vector.scalar_tensor_tensor(out=xmix[:, 0, c, :], in0=sx[:, c, :],
                                                         scalar=cols_s[:, c, MAA_X:MAA_X + 1],
                                                         in1=xnT[:, c, 1:L + 1], op0=ALU.mult, op1=ALU.add)
                ins.then_inc(s_["xin_ready"], 1)

            slot_read = {1: ("lora_ready", 0), 2: ("dec1_ready", 0), 3: ("projk_ready", 0), 4: ("projv_ready", 0)}

            def f_mix(j):
                def run(b, par, n):
                    dve.wait_ge(s_["m2_ready"], NMIX * b + j + 1)
                    if j == 0:
                        if not first(b):
                            dve.wait_ge(s_["projg_ready"], b)
                    else:
                        dve.wait_ge(s_[slot_read[j][0]], b + 1)
                    for c in range(C):
                        at = MAA_STACK + MIXES[j]
                        ins = nc.vector.scalar_tensor_tensor(out=xmix[:, (j + 1) % 2, c, :],
                                                             in0=FA[:, c * L:(c + 1) * L],
                                                             scalar=cols_s[:, c, at:at + 1], in1=sx[:, c, :],
                                                             op0=ALU.add, op1=ALU.mult)
                    ins.then_inc(s_["mixm_ready"], 1)
                return run

            def f_g(b, par, n):
                dve.wait_ge(s_["gate_ready"], b + 1)
                nc.vector.scalar_tensor_tensor(out=gT[:, par, :], in0=gT[:, par, :], scalar=1.0, in1=FB[:],
                                               op0=ALU.add, op1=ALU.mult).then_inc(s_["g_ready"], 1)

            def decay_keys(par, m):
                w = wT[:, par, :] if m == 1 else totals(m)
                k = blocks(kT[:, par, :], m)[:, :, 0, :]
                return nc.vector.tensor_tensor(k, k, spread(blocks(w, 1)[:, :, 1, :], 2, m), ALU.mult)

            def decay_receptances(par, m):
                w = wT[:, par, :] if m == 1 else totals(m)
                r = blocks(rT[:, par, :], m)[:, :, 1, :]
                return nc.vector.tensor_tensor(r, r, spread(blocks(w, 1)[:, :, 0, :], 2, m), ALU.mult)

            def decay_totals(par, m):
                w = wT[:, par, :] if m == 1 else totals(m)
                return nc.vector.tensor_tensor(totals(2 * m), blocks(w, 1)[:, :, 0, 0], blocks(w, 1)[:, :, 1, 0],
                                               ALU.mult)

            def b_direct(i):
                m, c0, nc_ = DIRECT[i]
                src = BA if i % 2 == 0 else BB
                cl = slice(c0 * L, (c0 + nc_) * L)

                def run(b, par, n):
                    if m == 0:
                        dve.wait_ge(s_["v_ready"], b + 1)
                        dve.wait_ge(s_["score_ready"], ND * b + 1)
                        if not first(b):
                            dve.wait_ge(s_["attT_ready"], b)
                        nc.vector.tensor_tensor(acc[:], src[:], vT[:, par, :], ALU.mult).then_inc(s_["q_ready"], 1)
                        return
                    v = blocks(vT[:, par, cl], m)[:, :, 0, :]
                    a = blocks(acc[:, cl], m)[:, :, 1, :]
                    if m == 1:
                        dve.wait_ge(s_["w_ready"], b + 1)
                    dve.wait_ge(s_["p_ready"], ND * b + i + 1)
                    if c0 + nc_ == C:
                        if m > 1:
                            dve.wait_ge(s_["step_ready"], 7 * b + m.bit_length() - 1)
                        decay_totals(par, m)
                        decay_keys(par, m)
                        decay_receptances(par, m).then_inc(s_["step_ready"], 1)
                    dve.wait_ge(s_["score_ready"], ND * b + i + 1)
                    if m == 1:
                        nc.vector.tensor_tensor(qb[:, 0:512], src[:, 0:512], v.rearrange("p n m -> p (n m)"),
                                                ALU.mult).then_inc(s_["q_ready"], 1)
                        dve.wait_ge(s_["q_ready"], ND * b + i + 1)
                        add = qb[:, 0:512]
                    else:
                        nc.vector.tensor_tensor(qb.rearrange("p (n i j) -> p n i j", i=m, j=m),
                                                src[:].rearrange("p (n i j) -> p n i j", i=m, j=m),
                                                spread(v.unsqueeze(2), 2, m), ALU.mult).then_inc(s_["q_ready"], 1)
                        dve.wait_ge(s_["q_ready"], ND * b + i + 1)
                        add = qs[:, 0:1024 // m]
                        nc.vector.tensor_reduce(add, qb.rearrange("p (n j) -> p n j", j=m), AX.X,
                                                ALU.add).then_inc(s_["qs_ready"], 1)
                        dve.wait_ge(s_["qs_ready"], (ND - 2) * b + i - 1)
                    nc.vector.tensor_tensor(a, a, add.rearrange("p (n m) -> p n m", m=m),
                                            ALU.add).then_inc(s_["acc_ready"], 1)
                    dve.wait_ge(s_["acc_ready"], (ND - 1) * b + i)
                return run

            def b_ktok(l):
                m = LEVELS[l]

                def run(b, par, n):
                    if m == P:
                        return
                    dve.wait_ge(s_["step_ready"], 7 * b + 4 + l)
                    dve.wait_ge(s_["ktokT_ready"], 4 * b + l + 1)
                    decay_totals(par, m)
                    decay_keys(par, m).then_inc(s_["step_ready"], 1)
                return run

            def b_kv(q):
                m = STATE[q][0]
                width = 512 if m == P else 1024

                def run(b, par, n):
                    dve.wait_ge(s_["kv_ready"], NS * b + q + 1)
                    if q >= 2:
                        dve.wait_ge(s_["applied"], NS * b + q - 1)
                    nc.vector.tensor_tensor(sring[:, q % 2, 0:width].rearrange("p (n k) -> p n k", k=P),
                                            BA[:, 0:width].rearrange("p (n k) -> p n k", k=P),
                                            spread(hm_s[:, :].unsqueeze(1), 1, width // P),
                                            ALU.mult).then_inc(s_["s_ready"], 1)
                return run

            def b_apply(q):
                m = STATE[q][0]
                l = LEVELS.index(m)

                def run(b, par, n):
                    if q + 1 < NS and STATE[q + 1][0] == m:
                        return
                    dve.wait_ge(s_["applied"], NS * b + q + 1)
                    dve.wait_ge(s_["step_ready"], 7 * b + 4 + l)
                    if l:
                        dve.wait_ge(s_["rstep_ready"], 4 * b + l)
                    ins = decay_receptances(par, m)
                    ins.then_inc(s_["rstep_ready"], 1)
                return run

            def b_s0(b, par, n):
                dve.wait_ge(s_["o_ready"], b + 1)
                nc.vector.tensor_tensor(acc[:], BB[:], acc[:], ALU.add).then_inc(s_["att_ready"], 1)

            def heads(ap):
                return ap.rearrange("p (h s) -> p h s", s=S)

            def b_att(b, par, n):
                dve.wait_ge(s_["attT_ready"], b + 1)
                nc.vector.tensor_reduce(gsum[:], heads(BA[:]), AX.X, ALU.add).then_inc(s_["gsum_ready"], 1)
                dve.wait_ge(s_["gsum_ready"], b + 1)
                cf = cen[:, :, :].rearrange("p t e -> p (t e)")
                nc.vector.scalar_tensor_tensor(out=heads(cf), in0=spread(gsum[:, :].unsqueeze(2), 2, S),
                                               scalar=-1.0 / S, in1=heads(BA[:]), op0=ALU.mult,
                                               op1=ALU.add).then_inc(s_["cen_ready"], 1)
                dve.wait_ge(s_["sq_ready"], b + 1)
                nc.vector.tensor_reduce(gvar[:], heads(sq.rearrange("p t e -> p (t e)")), AX.X,
                                        ALU.add).then_inc(s_["gvar_ready"], 1)

            def b_gn(b, par, n):
                dve.wait_ge(s_["y1_ready"], b + 1)
                dve.wait_ge(s_["g_ready"], b + 1)
                yf = yb.rearrange("p c l -> p (c l)")
                nc.vector.scalar_tensor_tensor(out=yf, in0=yf, scalar=0.5, in1=gT[:, par, :], op0=ALU.mult,
                                               op1=ALU.mult).then_inc(s_["y_ready"], 1)

            def b_wo(b, par, n):
                dve.wait_ge(s_["wo_ready"], b + 1)
                nc.vector.tensor_tensor(x1[:, :, :].rearrange("p t e -> p (t e)"), BA[:],
                                        xt[:, par].rearrange("p t e -> p (t e)"), ALU.add).then_inc(s_["x1_ready"], 1)
                dve.wait_ge(s_["x1_ready"], b + 1)
                stats(x1, st2, s_["st2_ready"], mv2, s_["mv2_ready"], b)
                dve.wait_ge(s_["rs2_ready"], b + 1)
                norm(xhat2, x1, mv2, rs2).then_inc(s_["xhat2_ready"], 1)

            def b_mix2(b, par, n):
                dve.wait_ge(s_["sx2_ready"], b + 1)
                for dst, at, ready in ((xr, FFN_MAA_R, "xr_ready"), (xk, FFN_MAA_K, "xk_ready")):
                    for c in range(C):
                        ins = nc.vector.scalar_tensor_tensor(out=dst[:, c, :], in0=sx2[:, c, :],
                                                             scalar=cols_s[:, c, at:at + 1],
                                                             in1=xn2T[:, c, 1:L + 1], op0=ALU.mult, op1=ALU.add)
                    ins.then_inc(s_[ready], 1)

            def b_out(b, par, n):
                dve.wait_ge(s_["fv_ready"], b + 1)
                rf = rr.rearrange("p t e -> p (t e)")
                nc.vector.scalar_tensor_tensor(out=rf, in0=rf, scalar=1.0, in1=BA[:], op0=ALU.add,
                                               op1=ALU.mult).then_inc(s_["mul_ready"], 1)
                dve.wait_ge(s_["mul_ready"], b + 1)
                nc.vector.scalar_tensor_tensor(out=outt.rearrange("p t e -> p (t e)"), in0=rf, scalar=0.5,
                                               in1=x1[:, :, :].rearrange("p t e -> p (t e)"), op0=ALU.mult,
                                               op1=ALU.add).then_inc(s_["out_ready"], 1)

            dve.wait_ge(c_loaded, 16 * 5)
            steps = dict(f_stats=f_stats, f_norm=f_norm, f_lora=f_lora, f_g=f_g, b_s0=b_s0, b_att=b_att, b_gn=b_gn,
                         b_wo=b_wo, b_mix2=b_mix2, b_out=b_out)
            steps.update({f"f_mix{j}": f_mix(j) for j in range(NMIX)})
            steps.update({f"b_direct{i}": b_direct(i) for i in range(ND)})
            steps.update({f"b_ktok{m}": b_ktok(l) for l, m in enumerate(LEVELS)})
            steps.update({f"b_kv{q}": b_kv(q) for q in range(NS)})
            steps.update({f"b_apply{q}": b_apply(q) for q in range(NS)})
            walk(dve, steps)


def kernel(**inputs):
    import concourse.bacc as bacc
    from concourse.bass_utils import run_bass_kernel_spmd

    a = {k.replace("L0_xattn_", ""): np.asarray(v) for k, v in inputs.items()}
    ctx = a["ctx_2048"]

    def tiles(w):
        return w.reshape(C, P, -1).transpose(1, 0, 2)

    vectors = np.concatenate([
        a["ln1_w"][None], a["ln1_b"][None], a["ln2_w"][None], a["ln2_b"][None], a["maa_x"][None], a["maa_stack"],
        a["time_decay"][None], a["faaaa"].reshape(1, E), a["gn_w"][None], a["gn_b"][None], a["ffn_maa_k"][None],
        a["ffn_maa_r"][None], ctx[:, 1], ctx[:, 0]])
    p = np.arange(P)
    tokmask = np.stack([(p // m == 2 * i) for m in LEVELS[:3] for i in range(P // (2 * m))], 1)
    arrays = dict(
        x=a["x"],
        cols=tiles(vectors.T),
        s0=ctx[:, 2:2 + S].reshape(B, C, P, S).transpose(2, 0, 1, 3),
        w1=tiles(a["maa_w1"]), w2a=a["maa_w2"][:4].reshape(P, E), w2b=a["maa_w2"][4],
        dw1=tiles(a["decay_w1"]), dw2=a["decay_w2"],
        wk=tiles(a["Wk"].T), wv=tiles(a["Wv"].T), wr=tiles(a["Wr"].T), wg=tiles(a["Wg"].T), wo=tiles(a["Wo"].T),
        fk=tiles(a["ffn_Wk"].T), fr=tiles(a["ffn_Wr"].T), fv=tiles(a["ffn_Wv"].T),
        ident=np.eye(P, dtype=np.float32),
        headmask=(p[:, None] // S == p[None, :] // S).astype(np.float32),
        tokmask=tokmask.astype(np.float32))
    arrays = {k: np.ascontiguousarray(v) for k, v in arrays.items()}
    nc = bacc.Bacc("TRN2", target_bir_lowering=False, num_devices=1)
    args = [nc.dram_tensor(k, v.shape, mybir.dt.from_np(v.dtype), kind="ExternalInput").ap()
            for k, v in arrays.items()]
    args.append(nc.dram_tensor("out", (B, L, E), F32, kind="ExternalOutput").ap())
    wkv_kernel(nc, *args)
    r = run_bass_kernel_spmd(nc, [arrays], core_ids=[0])
    return r.results[0]["out"]
```

```python
from contextlib import ExitStack

import numpy as np

import concourse.bass as bass
from concourse import mybir

ALU = mybir.AluOpType
ACT = mybir.ActivationFunctionType
AX = mybir.AxisListType
F32 = mybir.dt.float32

B, L, E, H = 8, 256, 512, 32
S = E // H
P = 128
C = E // P
T = L // P
HP = P // S
LORA, NMIX, DEC = 32, 5, 64
EPS = 1e-5
PAIRS = B // 2 - 1

(LN1_W, LN1_B, LN2_W, LN2_B, MAA_X, MAA_STACK, TIME_DECAY, FAAAA, GN_W, GN_B, FFN_MAA_K, FFN_MAA_R,
 PREV_ATT, PREV_FFN, NCOLS) = (0, 1, 2, 3, 4, 5, 10, 11, 12, 13, 14, 15, 16, 16 + B, 16 + 2 * B)

MIXES = (1, 0, 2, 3, 4)

DIRECT = ((0, 0, 4), (1, 0, 4), (2, 0, 4), (4, 0, 2), (4, 2, 2), (8, 0, 1), (8, 1, 1), (8, 2, 1), (8, 3, 1))
ND = len(DIRECT)
LEVELS = (16, 32, 64, 128)
STATE = tuple((m, tuple((c, i) for c in range(C) for i in range(L // (2 * m)))[4 * k:4 * k + 4])
              for m in LEVELS for k in range(C * L // (8 * m)))
NS = len(STATE)
LEVEL_AT = {m: [p[0] for p in STATE].index(m) for m in LEVELS}
KEYS_AT = {16: 0, 32: 0, 64: 2, 128: 3}

SCHEDULE = (
    "b_prod0", "b_prod1", "b_step1", "f_stats", "b_score0", "b_sum0", "f_norm", "b_prod2", "b_score1", "b_sum1",
    "b_step2", "b_prod3", "b_prod4", "f_sx", "b_score2", "b_step4", "b_sum2", "f_xin", "b_prod5", "b_score3",
    "b_sum3", "b_score4", "b_sum4", "b_prod6", "f_lora", "b_score5", "b_sum5", "b_prod7", "f_m20", "b_score6",
    "f_mix0", "b_sum6", "f_add0", "b_prod8", "b_step8", "f_m21", "b_score7", "b_sum7", "f_dec1", "f_mix1", "f_add1",
    "b_score8", "b_sum8", "b_s0bd",
    "b_vtok", "b_ktok16", "f_m22", "f_mix2", "f_add2", "b_kv0", "b_kv1", "b_kv2", "b_apply0", "b_kv3", "b_apply1",
    "b_kv4", "b_apply2", "b_kv5", "b_apply3", "b_kv6", "b_apply4", "b_kv7", "b_apply5", "b_apply6", "b_ktok32",
    "b_apply7", "b_rstep16", "f_m23", "f_mix3", "f_add3", "b_kv8", "b_kv9", "b_kv10", "b_apply8", "b_kv11", "b_apply9",
    "b_apply10", "b_ktok64", "b_apply11", "b_rstep32", "f_dec2", "b_kv12", "b_kv13", "b_apply12", "b_ktok128", "b_apply13", "b_rstep64",
    "b_kv14", "b_apply14", "b_rstep128", "b_s0", "b_att", "f_k", "f_v", "b_gn", "f_m24", "f_mix4", "f_add4", "b_wo", "b_norm2",
    "f_r", "b_ffn", "b_out", "f_g",
)


def spread(ap, axis, n):
    shape = list(ap.shape)
    shape[axis] = n
    return ap.broadcast_to(shape)


def wkv_kernel(nc, x, cols, s0, w1, w2a, w2b, dw1, dw2, wk, wv, wr, wg, wo, fk, fr, fv, ident, headmask, tokmask, out):
    with ExitStack() as ctx:
        def sb(name, shape):
            return ctx.enter_context(nc.sbuf_tensor(name, shape, F32))

        def sem(name):
            return ctx.enter_context(nc.semaphore(name))

        cols_s = sb("cols_s", [P, C, NCOLS])
        s0_s = sb("s0_s", [P, B, C, S])
        ident_s = sb("ident_s", [P, P])
        hm_s = sb("hm_s", [P, P])
        tm_s = sb("tm_s", [P, 7])
        u_s = sb("u_s", [P, C, P])
        w1_s = sb("w1_s", [P, C, NMIX * LORA])
        w2a_s = sb("w2a_s", [P, E])
        w2b_s = sb("w2b_s", [LORA, E])
        dw1_s = sb("dw1_s", [P, C, DEC])
        dw2_s = sb("dw2_s", [DEC, E])
        big = {n: sb(n + "_s", [P, C, E]) for n in ("wk", "wv", "wr", "wg", "wo", "fk", "fr", "fv")}
        pause = sb("pause", [P, 1])
        eps_s = sb("eps_s", [P, T * H])
        half_s = sb("half_s", [P, T * H])

        xt = sb("xt", [P, 2, T, E])
        st1 = sb("st1", [P, T, 6])
        mv1 = sb("mv1", [P, T, 2])
        ve1 = sb("ve1", [P, T])
        rs1 = sb("rs1", [P, T])
        xhat = sb("xhat", [P, T, E])
        xnT = sb("xnT", [P, C, L + 1])
        sx = sb("sx", [P, C, L])
        xmix = sb("xmix", [P, 3, C, L])
        thA = sb("thA", [P, L])
        thB = sb("thB", [LORA, L])
        dech = sb("dech", [DEC, L])
        rT, kT, vT, wT, gT = (sb(n, [P, 2, C * L]) for n in ("rT", "kT", "vT", "wT", "gT"))

        pp = sb("pp", [P, 3, 1024])
        acc = sb("acc", [P, C * L])
        tot = sb("tot", [P, 1024])
        vtok = sb("vtok", [P, T, E])
        kexp = sb("kexp", [P, 4, T, E])
        sring = sb("sring", [P, 4, 512])
        s0bd = sb("s0bd", [P, C, HP, S])
        gsum = sb("gsum", [P, T * H])
        gvar = sb("gvar", [P, T * H])
        gve = sb("gve", [P, T * H])
        grs = sb("grs", [P, T * H])
        cen = vtok
        x1 = tot[:, :].rearrange("p (t e) -> p t e", t=T)
        st2 = sb("st2", [P, T, 6])
        mv2 = sb("mv2", [P, T, 2])
        ve2 = sb("ve2", [P, T])
        rs2 = sb("rs2", [P, T])
        xn2T = sring[:, :, :].rearrange("p q k -> p (q k)")[:, 0:C * (L + 1)].rearrange("p (c l) -> p c l", c=C)
        qb = kexp[:, 0, :, :].rearrange("p t e -> p (t e)")
        qs = kexp[:, 1, 0, :]
        xhat2 = cen
        xk = kexp[:, 0, :, :].rearrange("p t e -> p (t e)").rearrange("p (c l) -> p c l", c=C)
        xr = kexp[:, 1, :, :].rearrange("p t e -> p (t e)").rearrange("p (c l) -> p c l", c=C)
        kk = xk
        rr = kexp[:, 2, :, :]
        sq = rr
        yb = kexp[:, 3, :, :].rearrange("p t e -> p (t e)").rearrange("p (c l) -> p c l", c=C)
        sx2 = yb
        outt = kexp[:, 3, :, :]

        FA, FB, BA, BB = (ctx.enter_context(nc.psum_tensor(n, [P, 1024], F32)) for n in ("FA", "FB", "BA", "BB"))

        c_loaded = sem("c_loaded")
        w_loaded = {n: sem(n + "_loaded") for n in
                    ("w1", "w2", "dw", "wk", "wv", "wr", "wg", "wo", "fk", "fr", "fv")}
        x_loaded = [sem("x_loaded0"), sem("x_loaded1")]
        half_ready = sem("half_ready")
        u_ready = sem("u_ready")
        names = (
            "st1_ready mv1_ready ve1_ready rs1_ready xhat_ready xhatT_ready xnT_ready sx_ready xin_ready lora_ready "
            "th_ready m2_ready mixm_ready mix_ready dech_ready dec1_ready dec2_ready wexp_ready w_ready "
            "k_ready v_ready r_ready gate_ready g_ready projk_ready projv_ready projr_ready projg_ready "
            "p_ready score_ready q_ready qs_ready acc_ready step_ready vtokT_ready vtok_ready ktokT_ready ktok_ready "
            "kv_ready s_ready rstep_ready applied s0bd_ready o_ready att_ready attT_ready gsum_ready cen_ready sq_ready gvar_ready "
            "gve_ready grs_ready nrm_ready nrmT_ready y1_ready y_ready wo_ready x1_ready st2_ready mv2_ready ve2_ready "
            "rs2_ready xhat2_ready xhat2T_ready xn2T_ready sx2_ready xk_ready xr_ready fr_ready rr_ready fk_ready "
            "relu_ready kk_ready fv_ready mul_ready out_ready stored").split()
        s_ = {n: sem(n) for n in names}

        def blocks(ap, m):
            return ap.rearrange("p (n two m) -> p n two m", two=2, m=m)

        def totals(m):
            at = sum(C * L // q for q in (2, 4, 8, 16, 32, 64, 128) if q < m)
            return tot[:, at:at + C * L // m]

        block = ctx.enter_context(nc.Block())

        def walk(eng, steps):
            def run(front, back):
                for name in SCHEDULE:
                    which = front if name[0] == "f" else back
                    if name in steps and which is not None:
                        steps[name](*which)
            run((0, 0, 0), None)
            run((1, 1, 0), (0, 0, 0))
            with eng.Fori(0, PAIRS) as j:
                run((2 * j + 2, 0, j + 1), (2 * j + 1, 1, j))
                run((2 * j + 3, 1, j + 1), (2 * j + 2, 0, j + 1))
            run(None, (B - 1, 1, B // 2 - 1))

        def first(b):
            return isinstance(b, int) and b == 0

        @block.sync
        def _(sp):
            def load_x(b, par):
                sp.dma_start(xt[:, par], x[b].rearrange("(t p) e -> p t e", p=P)).then_inc(x_loaded[par], 16)

            load_x(0, 0)
            for dst, src in ((cols_s, cols), (ident_s, ident), (hm_s, headmask), (tm_s, tokmask), (s0_s, s0)):
                sp.dma_start(dst[:], src).then_inc(c_loaded, 16)
            sp.dma_start(w1_s[:], w1).then_inc(w_loaded["w1"], 16)
            sp.dma_start(w2a_s[:], w2a).then_inc(w_loaded["w2"], 16)
            sp.dma_start(w2b_s[:], w2b).then_inc(w_loaded["w2"], 16)
            sp.dma_start(dw1_s[:], dw1).then_inc(w_loaded["dw"], 16)
            sp.dma_start(dw2_s[:], dw2).then_inc(w_loaded["dw"], 16)
            load_x(1, 1)
            for n, src in (("wk", wk), ("wv", wv), ("wr", wr), ("wg", wg), ("wo", wo), ("fr", fr), ("fk", fk),
                           ("fv", fv)):
                sp.dma_start(big[n][:], src).then_inc(w_loaded[n], 16)

            def store(b):
                sp.wait_ge(s_["out_ready"], b + 1)
                sp.dma_start(out[b].rearrange("(t p) e -> p t e", p=P), outt).then_inc(s_["stored"], 16)

            def reload(b, par):
                sp.wait_ge(s_["x1_ready"], b - 1)
                load_x(b, par)

            reload(2, 0)
            store(0)
            with sp.Fori(0, PAIRS - 1) as j:
                reload(2 * j + 3, 1)
                store(2 * j + 1)
                reload(2 * j + 4, 0)
                store(2 * j + 2)
            reload(B - 1, 1)
            store(B - 3)
            store(B - 2)
            store(B - 1)
            sp.wait_ge(s_["stored"], 16 * B)

        @block.gpsimd
        def _(pool):
            nc.gpsimd.memset(half_s[:], -0.5).then_inc(half_ready, 1)
            nc.gpsimd.memset(eps_s[:], EPS).then_inc(half_ready, 1)
            pool.wait_ge(half_ready, 2)
            pool.wait_ge(c_loaded, 16 * 5)
            for c in range(C):
                nc.gpsimd.tensor_tensor(u_s[:, c, :], hm_s[:], spread(cols_s[:, c, FAAAA:FAAAA + 1], 1, P),
                                        ALU.mult).then_inc(u_ready, 1)

            def inverse_root(mv_ready, mv, ve, ve_ready, rs, rs_ready, b):
                pool.wait_ge(mv_ready, b + 1)
                nc.gpsimd.tensor_tensor(ve[:], mv, eps_s[:, 0:T], ALU.add).then_inc(ve_ready, 1)
                pool.wait_ge(ve_ready, b + 1)
                nc.gpsimd.tensor_tensor(rs[:], ve[:], half_s[:, 0:T], ALU.pow).then_inc(rs_ready, 1)

            def f_stats(b, par, n):
                inverse_root(s_["mv1_ready"], mv1[:, :, 1], ve1, s_["ve1_ready"], rs1, s_["rs1_ready"], b)

            def f_sx(b, par, n):
                pool.wait_ge(s_["xnT_ready"], b + 1)
                if not first(b):
                    pool.wait_ge(s_["mixm_ready"], NMIX * b)
                nc.gpsimd.tensor_tensor(sx[:], xnT[:, :, 0:L], xnT[:, :, 1:L + 1],
                                        ALU.subtract).then_inc(s_["sx_ready"], 1)

            def f_add(j):
                def run(b, par, n):
                    pool.wait_ge(s_["mixm_ready"], NMIX * b + j + 1)
                    slot = xmix[:, j % 3]
                    nc.gpsimd.tensor_tensor(slot, slot, xnT[:, :, 1:L + 1], ALU.add).then_inc(s_["mix_ready"], 1)
                return run

            def b_prod(i):
                m, c0, nc_ = DIRECT[i]

                def run(b, par, n):
                    r, k = rT[:, par, c0 * L:(c0 + nc_) * L], kT[:, par, c0 * L:(c0 + nc_) * L]
                    if m == 0:
                        pool.wait_ge(s_["r_ready"], b + 1)
                        pool.wait_ge(s_["k_ready"], b + 1)
                    elif m > 1 and c0 == 0:
                        pool.wait_ge(s_["step_ready"], 7 * b + {2: 1, 4: 2, 8: 3}[m])
                    if i >= 3 or not first(b):
                        pool.wait_ge(s_["score_ready"], ND * b + i - 2)
                    slot = pp[:, i % 3, :]
                    if m == 0:
                        ins = nc.gpsimd.tensor_tensor(slot, r, k, ALU.mult)
                    elif m == 1:
                        ins = nc.gpsimd.tensor_tensor(slot[:, 0:C * L // 2], blocks(r, 1)[:, :, 1, 0],
                                                      blocks(k, 1)[:, :, 0, 0], ALU.mult)
                    else:
                        ins = nc.gpsimd.tensor_tensor(
                            slot.rearrange("p (n i j) -> p n i j", i=m, j=m),
                            spread(blocks(r, m)[:, :, 1, :].unsqueeze(3), 3, m),
                            spread(blocks(k, m)[:, :, 0, :].unsqueeze(2), 2, m), ALU.mult)
                    ins.then_inc(s_["p_ready"], 1)
                return run

            def b_s0bd(b, par, n):
                if not first(b):
                    pool.wait_ge(s_["o_ready"], b)
                nc.gpsimd.tensor_tensor(
                    s0bd[:], spread(s0_s[:, b, :, :].unsqueeze(2), 2, HP),
                    spread(hm_s[:, :].rearrange("p (h s) -> p h s", h=HP).unsqueeze(1), 1, C),
                    ALU.mult).then_inc(s_["s0bd_ready"], 1)

            def b_gn(b, par, n):
                pool.wait_ge(s_["gvar_ready"], b + 1)
                nc.gpsimd.tensor_tensor(gve[:], gvar[:], eps_s[:], ALU.add).then_inc(s_["gve_ready"], 1)
                pool.wait_ge(s_["gve_ready"], b + 1)
                nc.gpsimd.tensor_tensor(grs[:], gve[:], half_s[:], ALU.pow).then_inc(s_["grs_ready"], 1)
                pool.wait_ge(s_["grs_ready"], b + 1)
                c3 = cen[:, :, :].rearrange("p t e -> p (t e)").rearrange("p (h s) -> p h s", s=S)
                nc.gpsimd.tensor_tensor(c3, c3, spread(grs[:, :].unsqueeze(2), 2, S),
                                        ALU.mult).then_inc(s_["nrm_ready"], 1)

            def b_wo(b, par, n):
                inverse_root(s_["mv2_ready"], mv2[:, :, 1], ve2, s_["ve2_ready"], rs2, s_["rs2_ready"], b)

            steps = dict(f_stats=f_stats, f_sx=f_sx, b_s0bd=b_s0bd, b_gn=b_gn, b_wo=b_wo)
            steps.update({f"f_add{j}": f_add(j) for j in range(NMIX)})
            steps.update({f"b_prod{i}": b_prod(i) for i in range(ND)})
            walk(pool, steps)

        @block.tensor
        def _(pe):
            def transpose_tokens(dst, src):
                for t in range(T):
                    for c in range(C):
                        ins = nc.tensor.transpose(dst[:, t * E + c * P:t * E + (c + 1) * P],
                                                  src[:, c * L + t * P:c * L + (t + 1) * P], ident_s[:])
                return ins

            def transpose_channels(dst, src):
                for c in range(C):
                    for t in range(T):
                        ins = nc.tensor.transpose(dst[:, c * L + t * P:c * L + (t + 1) * P],
                                                  src[:, t, c * P:(c + 1) * P], ident_s[:])
                return ins

            def project(dst, weight, src):
                for c in range(C):
                    for q in range(C):
                        ins = nc.tensor.matmul(dst[:, c * L:(c + 1) * L], weight[:, q, c * P:(c + 1) * P],
                                               src[:, q, :], start=(q == 0), stop=(q == C - 1))
                return ins

            def project_tokens(dst, weight, src):
                for t in range(T):
                    for q in range(C):
                        ins = nc.tensor.matmul(dst[:, t * E:(t + 1) * E], src[:, q, t * P:(t + 1) * P],
                                               weight[:, q, :], start=(q == 0), stop=(q == C - 1))
                return ins

            def loaded(name, n=16):
                pe.wait_ge(w_loaded[name], n)

            def f_norm(b, par, n):
                if first(b):
                    pe.wait_ge(c_loaded, 16 * 5)
                pe.wait_ge(s_["xhat_ready"], b + 1)
                if not first(b):
                    pe.wait_ge(s_["mixm_ready"], NMIX * b)
                transpose_channels(FA, xhat).then_inc(s_["xhatT_ready"], 1)

            def f_lora(b, par, n):
                loaded("w1")
                pe.wait_ge(s_["xin_ready"], b + 1)
                if not first(b):
                    pe.wait_ge(s_["g_ready"], b)
                    pe.wait_ge(s_["gate_ready"], b)
                for q in range(C):
                    nc.tensor.matmul(FB[:, 0:L], w1_s[:, q, 0:P], xmix[:, 2, q, :], start=(q == 0), stop=(q == C - 1))
                for q in range(C):
                    ins = nc.tensor.matmul(FB[0:LORA, 512:512 + L], w1_s[:, q, P:P + LORA], xmix[:, 2, q, :],
                                           start=(q == 0), stop=(q == C - 1))
                ins.then_inc(s_["lora_ready"], 1)

            def f_m2(j):
                i = MIXES[j]

                def run(b, par, n):
                    if j == 0:
                        loaded("w2", 32)
                        pe.wait_ge(s_["th_ready"], 2 * b + 2)
                    else:
                        pe.wait_ge(s_["mixm_ready"], NMIX * b + j)
                    for c in range(C):
                        if i < 4:
                            lhs, rhs = w2a_s[32 * i:32 * i + 32, c * P:(c + 1) * P], thA[32 * i:32 * i + 32, :]
                        else:
                            lhs, rhs = w2b_s[:, c * P:(c + 1) * P], thB[:, :]
                        ins = nc.tensor.matmul(FA[:, c * L:(c + 1) * L], lhs, rhs, start=True, stop=True)
                    ins.then_inc(s_["m2_ready"], 1)
                return run

            def f_dec1(b, par, n):
                loaded("dw", 32)
                pe.wait_ge(s_["mix_ready"], NMIX * b + 1)
                pe.wait_ge(s_["th_ready"], 2 * b + 2)
                for q in range(C):
                    ins = nc.tensor.matmul(FB[0:DEC, 0:L], dw1_s[:, q, :], xmix[:, 0, q, :],
                                           start=(q == 0), stop=(q == C - 1))
                ins.then_inc(s_["dec1_ready"], 1)

            def f_dec2(b, par, n):
                pe.wait_ge(s_["dech_ready"], b + 1)
                for c in range(C):
                    ins = nc.tensor.matmul(FB[:, c * L:(c + 1) * L], dw2_s[:, c * P:(c + 1) * P], dech[:],
                                           start=True, stop=True)
                ins.then_inc(s_["dec2_ready"], 1)

            def f_proj(read, j, weight, done):
                def run(b, par, n):
                    loaded(weight)
                    pe.wait_ge(s_["mix_ready"], NMIX * b + j + 1)
                    pe.wait_ge(s_[read], b + 1)
                    project(FB, big[weight], xmix[:, j % 3]).then_inc(s_[done], 1)
                return run

            def b_score(i):
                m, c0, nc_ = DIRECT[i]
                dst = BA if i % 2 == 0 else BB

                def run(b, par, n):
                    pe.wait_ge(s_["p_ready"], ND * b + i + 1)
                    if i == 0:
                        pe.wait_ge(u_ready, C)
                        pe.wait_ge(s_["out_ready"], b)
                    elif i == 1:
                        if not first(b):
                            pe.wait_ge(s_["relu_ready"], b)
                    else:
                        pe.wait_ge(s_["q_ready"], ND * b + i - 1)
                    slot = pp[:, i % 3, :]
                    if m == 0:
                        for c in range(C):
                            ins = nc.tensor.matmul(dst[:, c * L:(c + 1) * L], u_s[:, c, :], slot[:, c * L:(c + 1) * L],
                                                   start=True, stop=True)
                    else:
                        for h in range(1 if m == 1 else 2):
                            ins = nc.tensor.matmul(dst[:, h * 512:(h + 1) * 512], hm_s[:],
                                                   slot[:, h * 512:(h + 1) * 512], start=True, stop=True)
                    ins.then_inc(s_["score_ready"], 1)
                return run

            def b_vtok(b, par, n):
                pe.wait_ge(s_["v_ready"], b + 1)
                pe.wait_ge(s_["q_ready"], ND * b + ND)
                transpose_tokens(BA, vT[:, par, :]).then_inc(s_["vtokT_ready"], 1)

            def b_ktok(l):
                m = LEVELS[l]

                def run(b, par, n):
                    pe.wait_ge(s_["step_ready"], 7 * b + (4, 5, 6, 7)[l])
                    if l == 0:
                        pe.wait_ge(s_["vtok_ready"], b + 1)
                    else:
                        pe.wait_ge(s_["s_ready"], NS * b + LEVEL_AT[m])
                    src = kT[:, par, :]
                    if m < P:
                        ins = transpose_tokens(BA, src)
                    else:
                        for c in range(C):
                            ins = nc.tensor.transpose(BA[:, c * P:(c + 1) * P], src[:, c * L:c * L + P], ident_s[:])
                    ins.then_inc(s_["ktokT_ready"], 1)
                return run

            def b_kv(q):
                m, pairs = STATE[q]
                bank, per = BA[:, q % 2 * 512:], max(P // (2 * m), 1)

                def run(b, par, n):
                    pe.wait_ge(s_["ktok_ready"], 4 * b + LEVELS.index(m) + 1)
                    if q >= LEVEL_AT[m] + 2:
                        pe.wait_ge(s_["s_ready"], NS * b + q - 1)
                    for j, (c, i) in enumerate(pairs):
                        ins = nc.tensor.matmul(bank[:, j * P:(j + 1) * P],
                                               kexp[:, KEYS_AT[m] + i % per, i // per, c * P:(c + 1) * P],
                                               vtok[:, i // per, c * P:(c + 1) * P], start=True, stop=True)
                    ins.then_inc(s_["kv_ready"], 1)
                return run

            def b_apply(q):
                m, pairs = STATE[q]

                def run(b, par, n):
                    if q == 0:
                        pe.wait_ge(s_["step_ready"], 7 * b + 4)
                    elif q == LEVEL_AT[m]:
                        pe.wait_ge(s_["rstep_ready"], 4 * b + LEVELS.index(m))
                    pe.wait_ge(s_["s_ready"], NS * b + q + 1)
                    for j, (c, i) in enumerate(pairs):
                        t0 = 2 * m * i + m
                        ins = nc.tensor.matmul(BB[:, c * L + t0:c * L + t0 + m], sring[:, q % 4, j * P:(j + 1) * P],
                                               rT[:, par, c * L + t0:c * L + t0 + m],
                                               start=(m == LEVELS[0] and c % 2 == 0 and i == 0), stop=False,
                                               skip_group_check=True)
                    ins.then_inc(s_["applied"], 1)
                return run

            def b_s0(b, par, n):
                pe.wait_ge(s_["rstep_ready"], 4 * b + 4)
                pe.wait_ge(s_["s0bd_ready"], b + 1)
                for c in range(C):
                    ins = nc.tensor.matmul(BB[:, c * L:(c + 1) * L],
                                           s0bd[:, c, :, :].rearrange("p h s -> p (h s)"),
                                           rT[:, par, c * L:(c + 1) * L], start=False, stop=True,
                                           skip_group_check=True)
                ins.then_inc(s_["o_ready"], 1)

            def b_att(b, par, n):
                pe.wait_ge(s_["att_ready"], b + 1)
                pe.wait_ge(s_["s_ready"], NS * b + NS)
                transpose_tokens(BA, acc[:, :]).then_inc(s_["attT_ready"], 1)

            def b_gn(b, par, n):
                pe.wait_ge(s_["nrm_ready"], b + 1)
                transpose_channels(BA, cen).then_inc(s_["nrmT_ready"], 1)

            def b_wo(b, par, n):
                loaded("wo")
                pe.wait_ge(s_["y_ready"], b + 1)
                project_tokens(BA, big["wo"], yb).then_inc(s_["wo_ready"], 1)

            def b_norm2(b, par, n):
                pe.wait_ge(s_["xhat2_ready"], b + 1)
                transpose_channels(BA, xhat2).then_inc(s_["xhat2T_ready"], 1)

            def b_ffn(b, par, n):
                loaded("fr")
                pe.wait_ge(s_["xr_ready"], b + 1)
                project_tokens(BA, big["fr"], xr).then_inc(s_["fr_ready"], 1)
                loaded("fk")
                pe.wait_ge(s_["xk_ready"], b + 1)
                project(BB, big["fk"], xk).then_inc(s_["fk_ready"], 1)

            def b_out(b, par, n):
                loaded("fv")
                pe.wait_ge(s_["rr_ready"], b + 1)
                pe.wait_ge(s_["kk_ready"], b + 1)
                project_tokens(BA, big["fv"], kk).then_inc(s_["fv_ready"], 1)

            steps = dict(f_norm=f_norm, f_lora=f_lora, f_dec1=f_dec1, f_dec2=f_dec2,
                         f_k=f_proj("wexp_ready", 1, "wk", "projk_ready"), f_v=f_proj("k_ready", 2, "wv", "projv_ready"),
                         f_r=f_proj("v_ready", 3, "wr", "projr_ready"), f_g=f_proj("r_ready", 4, "wg", "projg_ready"),
                         b_vtok=b_vtok, b_s0=b_s0, b_att=b_att, b_gn=b_gn, b_wo=b_wo, b_norm2=b_norm2,
                         b_ffn=b_ffn, b_out=b_out)
            steps.update({f"f_m2{j}": f_m2(j) for j in range(NMIX)})
            steps.update({f"b_score{i}": b_score(i) for i in range(ND)})
            steps.update({f"b_ktok{m}": b_ktok(l) for l, m in enumerate(LEVELS)})
            steps.update({f"b_kv{q}": b_kv(q) for q in range(NS)})
            steps.update({f"b_apply{q}": b_apply(q) for q in range(NS)})
            walk(pe, steps)

        @block.scalar
        def _(act):
            def col(i):
                return lambda c: cols_s[:, c, i:i + 1]

            def f_norm(b, par, n):
                if first(b):
                    act.wait_ge(c_loaded, 16 * 5)
                else:
                    act.wait_ge(s_["mix_ready"], NMIX * b)
                act.wait_ge(s_["xhatT_ready"], b + 1)
                nc.scalar.activation(xnT[:, :, 0:1], cols_s[:, :, bass.ds(PREV_ATT + b, 1)], ACT.Copy)
                for c in range(C):
                    ins = nc.scalar.activation(xnT[:, c, 1:L + 1], FA[:, c * L:(c + 1) * L], ACT.Identity,
                                               bias=col(LN1_B)(c), scale=col(LN1_W)(c))
                ins.then_inc(s_["xnT_ready"], 1)

            def f_lora(b, par, n):
                act.wait_ge(s_["lora_ready"], b + 1)
                if not first(b):
                    act.wait_ge(s_["m2_ready"], NMIX * b)
                nc.scalar.activation(thA[:], FB[:, 0:L], ACT.Tanh).then_inc(s_["th_ready"], 1)
                ins = nc.scalar.activation(thB[:], FB[0:LORA, 512:512 + L], ACT.Tanh)
                ins.then_inc(s_["th_ready"], 1)

            def f_dec1(b, par, n):
                act.wait_ge(s_["dec1_ready"], b + 1)
                nc.scalar.activation(dech[:], FB[0:DEC, 0:L], ACT.Tanh).then_inc(s_["dech_ready"], 1)

            def f_dec2(b, par, n):
                act.wait_ge(s_["dec2_ready"], b + 1)
                if not first(b):
                    act.wait_ge(s_["o_ready"], b - 1)
                for c in range(C):
                    ins = nc.scalar.activation(wT[:, par, c * L:(c + 1) * L], FB[:, c * L:(c + 1) * L], ACT.Exp,
                                               bias=col(TIME_DECAY)(c))
                ins.then_inc(s_["wexp_ready"], 1)
                act.wait_ge(s_["wexp_ready"], b + 1)
                nc.scalar.activation(wT[:, par, :], wT[:, par, :], ACT.Exp, scale=-1.0).then_inc(s_["w_ready"], 1)

            def f_proj(done, dst, ready):
                def run(b, par, n):
                    act.wait_ge(s_[done], b + 1)
                    if not first(b):
                        act.wait_ge(s_["o_ready"], b - 1)
                    nc.scalar.copy(dst[:, par, :], FB[:]).then_inc(s_[ready], 1)
                return run

            def f_g(b, par, n):
                act.wait_ge(s_["projg_ready"], b + 1)
                if not first(b):
                    act.wait_ge(s_["y_ready"], b - 1)
                nc.scalar.activation(gT[:, par, :], FB[:], ACT.Tanh, scale=0.5).then_inc(s_["gate_ready"], 1)

            def b_vtok(b, par, n):
                act.wait_ge(s_["vtokT_ready"], b + 1)
                nc.scalar.copy(vtok[:, :, :].rearrange("p t e -> p (t e)"), BA[:]).then_inc(s_["vtok_ready"], 1)

            def b_ktok(l):
                m = LEVELS[l]

                def run(b, par, n):
                    act.wait_ge(s_["ktokT_ready"], 4 * b + l + 1)
                    if l == 0:
                        if not first(b):
                            act.wait_ge(s_["stored"], 16 * b)
                        act.wait_ge(s_["acc_ready"], (ND - 1) * (b + 1))
                    else:
                        act.wait_ge(s_["kv_ready"], NS * b + LEVEL_AT[LEVELS[1]])
                    if m < P:
                        at = {16: 0, 32: 4, 64: 6}[m]
                        for i in range(P // (2 * m)):
                            ins = nc.scalar.activation(kexp[:, KEYS_AT[m] + i, :, :].rearrange("p t e -> p (t e)"), BA[:],
                                                       ACT.Copy, scale=tm_s[:, at + i:at + i + 1])
                    else:
                        ins = nc.scalar.copy(kexp[:, KEYS_AT[m], 0, :], BA[:, 0:E])
                    ins.then_inc(s_["ktok_ready"], 1)
                return run

            def b_att(b, par, n):
                act.wait_ge(s_["cen_ready"], b + 1)
                nc.scalar.activation(sq.rearrange("p t e -> p (t e)"),
                                     cen[:, :, :].rearrange("p t e -> p (t e)"), ACT.Square,
                                     scale=S ** -0.5).then_inc(s_["sq_ready"], 1)

            def b_gn(b, par, n):
                act.wait_ge(s_["nrmT_ready"], b + 1)
                for c in range(C):
                    ins = nc.scalar.activation(yb[:, c, :], BA[:, c * L:(c + 1) * L], ACT.Identity,
                                               bias=col(GN_B)(c), scale=col(GN_W)(c))
                ins.then_inc(s_["y1_ready"], 1)

            def b_norm2(b, par, n):
                act.wait_ge(s_["xhat2T_ready"], b + 1)
                nc.scalar.activation(xn2T[:, :, 0:1], cols_s[:, :, bass.ds(PREV_FFN + b, 1)], ACT.Copy)
                for c in range(C):
                    ins = nc.scalar.activation(xn2T[:, c, 1:L + 1], BA[:, c * L:(c + 1) * L], ACT.Identity,
                                               bias=col(LN2_B)(c), scale=col(LN2_W)(c))
                ins.then_inc(s_["xn2T_ready"], 1)

            def b_ffn(b, par, n):
                act.wait_ge(s_["fr_ready"], b + 1)
                nc.scalar.activation(rr.rearrange("p t e -> p (t e)"), BA[:], ACT.Tanh,
                                     scale=0.5).then_inc(s_["rr_ready"], 1)
                act.wait_ge(s_["fk_ready"], b + 1)
                kf = kk.rearrange("p c l -> p (c l)")
                nc.scalar.activation(kf, BB[:], ACT.Relu).then_inc(s_["relu_ready"], 1)
                act.wait_ge(s_["relu_ready"], b + 1)
                nc.scalar.activation(kf, kf, ACT.Square).then_inc(s_["kk_ready"], 1)

            steps = dict(f_norm=f_norm, f_lora=f_lora, f_dec1=f_dec1, f_dec2=f_dec2,
                         f_k=f_proj("projk_ready", kT, "k_ready"), f_v=f_proj("projv_ready", vT, "v_ready"),
                         f_r=f_proj("projr_ready", rT, "r_ready"), f_g=f_g,
                         b_vtok=b_vtok, b_att=b_att, b_gn=b_gn, b_norm2=b_norm2, b_ffn=b_ffn)
            steps.update({f"b_ktok{m}": b_ktok(l) for l, m in enumerate(LEVELS)})
            walk(act, steps)

        @block.vector
        def _(dve):
            def stats(src, st, st_ready, mv, mv_ready, b):
                for t in range(T):
                    ins = nc.vector.bn_stats(st[:, t, :], src[:, t, :])
                ins.then_inc(st_ready, 1)
                dve.wait_ge(st_ready, b + 1)
                nc.vector.memset(pause[:], 0.0)
                for t in range(T):
                    ins = nc.vector.bn_aggr(mv[:, t, :], st[:, t, :])
                ins.then_inc(mv_ready, 1)

            def norm(dst, src, mv, rs):
                for t in range(T):
                    ins = nc.vector.tensor_scalar(dst[:, t, :], src[:, t, :], mv[:, t, 0:1], rs[:, t:t + 1],
                                                  ALU.subtract, ALU.mult)
                return ins

            def f_stats(b, par, n):
                dve.wait_ge(x_loaded[par], 16 * n + 16)
                stats(xt[:, par], st1, s_["st1_ready"], mv1, s_["mv1_ready"], b)

            def f_norm(b, par, n):
                dve.wait_ge(s_["rs1_ready"], b + 1)
                if not first(b):
                    dve.wait_ge(s_["xhatT_ready"], b)
                norm(xhat, xt[:, par], mv1, rs1).then_inc(s_["xhat_ready"], 1)

            def f_xin(b, par, n):
                dve.wait_ge(s_["sx_ready"], b + 1)
                if not first(b):
                    dve.wait_ge(s_["projv_ready"], b)
                for c in range(C):
                    ins = nc.vector.scalar_tensor_tensor(out=xmix[:, 2, c, :], in0=sx[:, c, :],
                                                         scalar=cols_s[:, c, MAA_X:MAA_X + 1],
                                                         in1=xnT[:, c, 1:L + 1], op0=ALU.mult, op1=ALU.add)
                ins.then_inc(s_["xin_ready"], 1)

            slot_read = (("projr_ready", 1), ("projg_ready", 1), ("lora_ready", 0), ("dec1_ready", 0), ("projk_ready", 0))

            def f_mix(j):
                def run(b, par, n):
                    dve.wait_ge(s_["m2_ready"], NMIX * b + j + 1)
                    used, behind = slot_read[j]
                    if not (first(b) and behind):
                        dve.wait_ge(s_[used], b + 1 - behind)
                    for c in range(C):
                        at = MAA_STACK + MIXES[j]
                        ins = nc.vector.scalar_tensor_tensor(out=xmix[:, j % 3, c, :],
                                                             in0=FA[:, c * L:(c + 1) * L],
                                                             scalar=cols_s[:, c, at:at + 1], in1=sx[:, c, :],
                                                             op0=ALU.add, op1=ALU.mult)
                    ins.then_inc(s_["mixm_ready"], 1)
                return run

            def f_g(b, par, n):
                dve.wait_ge(s_["gate_ready"], b + 1)
                nc.vector.scalar_tensor_tensor(out=gT[:, par, :], in0=gT[:, par, :], scalar=1.0, in1=FB[:],
                                               op0=ALU.add, op1=ALU.mult).then_inc(s_["g_ready"], 1)

            def decay_keys(par, m):
                w = wT[:, par, :] if m == 1 else totals(m)
                k = blocks(kT[:, par, :], m)[:, :, 0, :]
                return nc.vector.tensor_tensor(k, k, spread(blocks(w, 1)[:, :, 1, :], 2, m), ALU.mult)

            def decay_receptances(par, m):
                w = wT[:, par, :] if m == 1 else totals(m)
                r = blocks(rT[:, par, :], m)[:, :, 1, :]
                return nc.vector.tensor_tensor(r, r, spread(blocks(w, 1)[:, :, 0, :], 2, m), ALU.mult)

            def decay_totals(par, m):
                w = wT[:, par, :] if m == 1 else totals(m)
                return nc.vector.tensor_tensor(totals(2 * m), blocks(w, 1)[:, :, 0, 0], blocks(w, 1)[:, :, 1, 0],
                                               ALU.mult)

            def b_step(m):
                last = max(i for i, piece in enumerate(DIRECT) if piece[0] == m)

                def run(b, par, n):
                    dve.wait_ge(s_["p_ready"], ND * b + last + 1)
                    if m == 1:
                        dve.wait_ge(s_["w_ready"], b + 1)
                        if not first(b):
                            dve.wait_ge(s_["out_ready"], b)
                    else:
                        dve.wait_ge(s_["step_ready"], 7 * b + m.bit_length() - 1)
                    decay_totals(par, m)
                    decay_keys(par, m)
                    decay_receptances(par, m).then_inc(s_["step_ready"], 1)
                return run

            def b_sum(i):
                m, c0, nc_ = DIRECT[i]
                src = BA if i % 2 == 0 else BB
                cl = slice(c0 * L, (c0 + nc_) * L)

                def run(b, par, n):
                    if m == 0:
                        dve.wait_ge(s_["v_ready"], b + 1)
                        dve.wait_ge(s_["score_ready"], ND * b + 1)
                        if not first(b):
                            dve.wait_ge(s_["attT_ready"], b)
                        nc.vector.tensor_tensor(acc[:], src[:], vT[:, par, :], ALU.mult).then_inc(s_["q_ready"], 1)
                        return
                    v = blocks(vT[:, par, cl], m)[:, :, 0, :]
                    a = blocks(acc[:, cl], m)[:, :, 1, :]
                    dve.wait_ge(s_["score_ready"], ND * b + i + 1)
                    if m == 1:
                        nc.vector.tensor_tensor(qb[:, 0:512], src[:, 0:512], v.rearrange("p n m -> p (n m)"),
                                                ALU.mult).then_inc(s_["q_ready"], 1)
                        dve.wait_ge(s_["q_ready"], ND * b + i + 1)
                        add = qb[:, 0:512]
                    else:
                        nc.vector.tensor_tensor(qb.rearrange("p (n i j) -> p n i j", i=m, j=m),
                                                src[:].rearrange("p (n i j) -> p n i j", i=m, j=m),
                                                spread(v.unsqueeze(2), 2, m), ALU.mult).then_inc(s_["q_ready"], 1)
                        dve.wait_ge(s_["q_ready"], ND * b + i + 1)
                        add = qs[:, 0:1024 // m]
                        nc.vector.tensor_reduce(add, qb.rearrange("p (n j) -> p n j", j=m), AX.X,
                                                ALU.add).then_inc(s_["qs_ready"], 1)
                        dve.wait_ge(s_["qs_ready"], (ND - 2) * b + i - 1)
                    nc.vector.tensor_tensor(a, a, add.rearrange("p (n m) -> p n m", m=m),
                                            ALU.add).then_inc(s_["acc_ready"], 1)
                    dve.wait_ge(s_["acc_ready"], (ND - 1) * b + i)
                return run

            def b_ktok(l):
                m = LEVELS[l]

                def run(b, par, n):
                    if m == P:
                        return
                    dve.wait_ge(s_["step_ready"], 7 * b + 4 + l)
                    dve.wait_ge(s_["ktokT_ready"], 4 * b + l + 1)
                    decay_totals(par, m)
                    decay_keys(par, m).then_inc(s_["step_ready"], 1)
                return run

            def b_kv(q):
                def run(b, par, n):
                    dve.wait_ge(s_["kv_ready"], NS * b + q + 1)
                    if q >= 4:
                        dve.wait_ge(s_["applied"], NS * b + q - 3)
                    nc.vector.tensor_tensor(sring[:, q % 4, :].rearrange("p (n k) -> p n k", k=P),
                                            BA[:, q % 2 * 512:q % 2 * 512 + 512].rearrange("p (n k) -> p n k", k=P),
                                            spread(hm_s[:, :].unsqueeze(1), 1, 4),
                                            ALU.mult).then_inc(s_["s_ready"], 1)
                return run

            def b_rstep(l):
                m = LEVELS[l]
                last = max(q for q in range(NS) if STATE[q][0] == m)

                def run(b, par, n):
                    dve.wait_ge(s_["applied"], NS * b + last + 1)
                    dve.wait_ge(s_["step_ready"], 7 * b + 4 + l)
                    if l:
                        dve.wait_ge(s_["rstep_ready"], 4 * b + l)
                    decay_receptances(par, m).then_inc(s_["rstep_ready"], 1)
                return run

            def b_s0(b, par, n):
                dve.wait_ge(s_["o_ready"], b + 1)
                nc.vector.tensor_tensor(acc[:], BB[:], acc[:], ALU.add).then_inc(s_["att_ready"], 1)

            def heads(ap):
                return ap.rearrange("p (h s) -> p h s", s=S)

            def b_att(b, par, n):
                dve.wait_ge(s_["attT_ready"], b + 1)
                nc.vector.tensor_reduce(gsum[:], heads(BA[:]), AX.X, ALU.add).then_inc(s_["gsum_ready"], 1)
                dve.wait_ge(s_["gsum_ready"], b + 1)
                cf = cen[:, :, :].rearrange("p t e -> p (t e)")
                nc.vector.scalar_tensor_tensor(out=heads(cf), in0=spread(gsum[:, :].unsqueeze(2), 2, S),
                                               scalar=-1.0 / S, in1=heads(BA[:]), op0=ALU.mult,
                                               op1=ALU.add).then_inc(s_["cen_ready"], 1)
                dve.wait_ge(s_["sq_ready"], b + 1)
                nc.vector.tensor_reduce(gvar[:], heads(sq.rearrange("p t e -> p (t e)")), AX.X,
                                        ALU.add).then_inc(s_["gvar_ready"], 1)

            def b_gn(b, par, n):
                dve.wait_ge(s_["y1_ready"], b + 1)
                dve.wait_ge(s_["g_ready"], b + 1)
                yf = yb.rearrange("p c l -> p (c l)")
                nc.vector.scalar_tensor_tensor(out=yf, in0=yf, scalar=0.5, in1=gT[:, par, :], op0=ALU.mult,
                                               op1=ALU.mult).then_inc(s_["y_ready"], 1)

            def b_wo(b, par, n):
                dve.wait_ge(s_["wo_ready"], b + 1)
                nc.vector.tensor_tensor(x1.rearrange("p t e -> p (t e)"), BA[:],
                                        xt[:, par].rearrange("p t e -> p (t e)"), ALU.add).then_inc(s_["x1_ready"], 1)
                dve.wait_ge(s_["x1_ready"], b + 1)
                stats(x1, st2, s_["st2_ready"], mv2, s_["mv2_ready"], b)
                dve.wait_ge(s_["rs2_ready"], b + 1)
                norm(xhat2, x1, mv2, rs2).then_inc(s_["xhat2_ready"], 1)

            def b_norm2(b, par, n):
                dve.wait_ge(s_["xn2T_ready"], b + 1)
                nc.vector.tensor_tensor(sx2, xn2T[:, :, 0:L], xn2T[:, :, 1:L + 1],
                                        ALU.subtract).then_inc(s_["sx2_ready"], 1)
                dve.wait_ge(s_["sx2_ready"], b + 1)
                for dst, at, ready in ((xr, FFN_MAA_R, "xr_ready"), (xk, FFN_MAA_K, "xk_ready")):
                    for c in range(C):
                        ins = nc.vector.scalar_tensor_tensor(out=dst[:, c, :], in0=sx2[:, c, :],
                                                             scalar=cols_s[:, c, at:at + 1],
                                                             in1=xn2T[:, c, 1:L + 1], op0=ALU.mult, op1=ALU.add)
                    ins.then_inc(s_[ready], 1)

            def b_out(b, par, n):
                dve.wait_ge(s_["fv_ready"], b + 1)
                rf = rr.rearrange("p t e -> p (t e)")
                nc.vector.scalar_tensor_tensor(out=rf, in0=rf, scalar=1.0, in1=BA[:], op0=ALU.add,
                                               op1=ALU.mult).then_inc(s_["mul_ready"], 1)
                dve.wait_ge(s_["mul_ready"], b + 1)
                nc.vector.scalar_tensor_tensor(out=outt.rearrange("p t e -> p (t e)"), in0=rf, scalar=0.5,
                                               in1=x1.rearrange("p t e -> p (t e)"), op0=ALU.mult,
                                               op1=ALU.add).then_inc(s_["out_ready"], 1)

            dve.wait_ge(c_loaded, 16 * 5)
            steps = dict(f_stats=f_stats, f_norm=f_norm, f_xin=f_xin, f_g=f_g, b_s0=b_s0, b_att=b_att, b_gn=b_gn,
                         b_wo=b_wo, b_norm2=b_norm2, b_out=b_out)
            steps.update({f"f_mix{j}": f_mix(j) for j in range(NMIX)})
            steps.update({f"b_sum{i}": b_sum(i) for i in range(ND)})
            steps.update({f"b_step{m}": b_step(m) for m in (1, 2, 4, 8)})
            steps.update({f"b_ktok{m}": b_ktok(l) for l, m in enumerate(LEVELS)})
            steps.update({f"b_kv{q}": b_kv(q) for q in range(NS)})
            steps.update({f"b_rstep{m}": b_rstep(l) for l, m in enumerate(LEVELS)})
            walk(dve, steps)


def kernel(**inputs):
    import concourse.bacc as bacc
    from concourse.bass_utils import run_bass_kernel_spmd

    a = {k.replace("L0_xattn_", ""): np.asarray(v) for k, v in inputs.items()}
    ctx = a["ctx_2048"]

    def tiles(w):
        return w.reshape(C, P, -1).transpose(1, 0, 2)

    vectors = np.concatenate([
        a["ln1_w"][None], a["ln1_b"][None], a["ln2_w"][None], a["ln2_b"][None], a["maa_x"][None], a["maa_stack"],
        a["time_decay"][None], a["faaaa"].reshape(1, E), a["gn_w"][None], a["gn_b"][None], a["ffn_maa_k"][None],
        a["ffn_maa_r"][None], ctx[:, 1], ctx[:, 0]])
    p = np.arange(P)
    tokmask = np.stack([(p // m == 2 * i) for m in LEVELS[:3] for i in range(P // (2 * m))], 1)
    arrays = dict(
        x=a["x"],
        cols=tiles(vectors.T),
        s0=ctx[:, 2:2 + S].reshape(B, C, P, S).transpose(2, 0, 1, 3),
        w1=tiles(a["maa_w1"]), w2a=a["maa_w2"][:4].reshape(P, E), w2b=a["maa_w2"][4],
        dw1=tiles(a["decay_w1"]), dw2=a["decay_w2"],
        wk=tiles(a["Wk"].T), wv=tiles(a["Wv"].T), wr=tiles(a["Wr"].T), wg=tiles(a["Wg"].T), wo=tiles(a["Wo"].T),
        fk=tiles(a["ffn_Wk"].T), fr=tiles(a["ffn_Wr"].T), fv=tiles(a["ffn_Wv"].T),
        ident=np.eye(P, dtype=np.float32),
        headmask=(p[:, None] // S == p[None, :] // S).astype(np.float32),
        tokmask=tokmask.astype(np.float32))
    arrays = {k: np.ascontiguousarray(v) for k, v in arrays.items()}
    nc = bacc.Bacc("TRN2", target_bir_lowering=False, num_devices=1)
    args = [nc.dram_tensor(k, v.shape, mybir.dt.from_np(v.dtype), kind="ExternalInput").ap()
            for k, v in arrays.items()]
    args.append(nc.dram_tensor("out", (B, L, E), F32, kind="ExternalOutput").ap())
    wkv_kernel(nc, *args)
    r = run_bass_kernel_spmd(nc, [arrays], core_ids=[0])
    return r.results[0]["out"]
```

```python
from contextlib import ExitStack

import numpy as np

import concourse.bass as bass
from concourse import mybir

ALU = mybir.AluOpType
ACT = mybir.ActivationFunctionType
AX = mybir.AxisListType
F32 = mybir.dt.float32

B, L, E, H = 8, 256, 512, 32
S = E // H
P = 128
C = E // P
T = L // P
HP = P // S
LORA, NMIX, DEC = 32, 5, 64
EPS = 1e-5
PAIRS = B // 2 - 1

(LN1_W, LN1_B, LN2_W, LN2_B, MAA_X, MAA_STACK, TIME_DECAY, FAAAA, GN_W, GN_B, FFN_MAA_K, FFN_MAA_R,
 PREV_ATT, PREV_FFN, NCOLS) = (0, 1, 2, 3, 4, 5, 10, 11, 12, 13, 14, 15, 16, 16 + B, 16 + 2 * B)

MIXES = (1, 0, 2, 3, 4)

DIRECT = ((0, 0, 4), (1, 0, 4), (2, 0, 4), (4, 0, 2), (4, 2, 2), (8, 0, 1), (8, 1, 1), (8, 2, 1), (8, 3, 1))
ND = len(DIRECT)
LAST_ODD = (ND - 2) // 2 * 2 + 1
LEVELS = (16, 32, 64, 128)
STATE = tuple((m, tuple((c, i) for c in range(C) for i in range(L // (2 * m)))[4 * k:4 * k + 4])
              for m in LEVELS for k in range(C * L // (8 * m)))
NS = len(STATE)
LEVEL_AT = {m: [p[0] for p in STATE].index(m) for m in LEVELS}
KEYS_AT = {16: 0, 32: 0, 64: 2, 128: 3}

ROOT = 12

ORDER = dict(
    tensor=dict(
        first="""
            warm6 f_norm warm14 f_lora warm4 f_m20 warm8 f_dec1 f_m21 warm2 f_dec2 f_m22 f_k0 f_k1
            f_k2 f_k3 f_m23 f_v0 f_v1 f_v2 f_v3 f_m24 f_r0 f_r1 f_r2 f_r3""".split(),
        main="""
            b_g0 b_g1 b_score0 b_score1 f_norm b_g2 b_g3 b_score2 b_score3 f_lora b_score4 f_m20
            b_score5 b_vtok f_m21 b_score6 b_score7 f_dec1 b_ktok16 b_score8 f_m22 b_kv0 b_kv1 b_kv2
            b_apply0 b_kv3 b_apply1 b_apply2 b_kv4 b_kv5 b_apply3 b_kv6 b_kv7 b_apply4 b_apply5
            b_ktok32 f_dec2 b_apply6 b_kv8 b_kv9 b_apply7 b_kv10 b_kv11 b_apply8 b_apply9 b_ktok64
            b_apply10 b_apply11 b_kv12 b_kv13 b_apply12 b_ktok128 b_apply13 b_kv14 b_s0 f_k0 b_apply14
            f_k1 b_att0 b_att1 f_k2 f_k3 f_m23 f_v0 f_v1 b_gn0 b_gn1 f_v2 f_v3 b_wo0 b_wo1
            f_m24 f_r0 b_norm20 b_norm21 f_r1 f_r2 f_r3 b_fk b_fr b_fv0 b_fv1""".split(),
        last="""
            b_score0 b_vtok b_score1 b_score2 b_score3 b_score4 b_score5 b_score6 b_score7 b_ktok16
            b_score8 b_kv0 b_kv1 b_kv2 b_apply0 b_kv3 b_apply1 b_kv4 b_kv5 b_apply2 b_apply3 b_kv6
            b_kv7 b_apply4 b_ktok32 b_apply5 b_apply6 b_apply7 b_kv8 b_kv9 b_kv10 b_kv11 b_apply8
            b_apply9 b_ktok64 b_apply10 b_apply11 b_kv12 b_kv13 b_apply12 b_ktok128 b_apply13 b_kv14 b_s0
            b_apply14 warm3 b_att0 b_att1 b_g0 b_g1 b_g2 b_g3 b_gn0 b_gn1 warm14 b_wo0 b_wo1
            warm8 b_norm20 b_norm21 warm20 b_fk b_fr b_fv0 b_fv1""".split()),
    vector=dict(
        main="""
            f_stats b_step1 f_norm b_step2 b_mul0 b_mul1 b_gate f_xin b_step4 b_mul2 b_mul3 b_red2
            f_mix0 f_mix1 b_mul4 b_red3 b_mul5 b_red4 b_red5 b_mul6 b_step8 b_mul7 b_red6 b_ktok16
            b_red7 b_mul8 b_red8 b_kv0 b_kv1 b_kv2 b_kv3 b_kv4 b_kv5 b_kv6 f_mix2 b_kv7 f_mix3 b_kv8
            b_kv9 b_ktok32 b_rstep16 b_kv10 b_kv11 b_ktok64 b_rstep32 b_kv12 b_kv13 b_rstep64 b_kv14
            b_o0 b_o1 b_cen0 b_cen1 b_var0 b_var1 b_root b_nrm0 b_nrm1 b_gn b_wo0 b_wo1
            b_xhat20 b_xhat21 f_mix4 b_norm2 b_out0 b_out1""".split(),
        last="""
            b_step1 b_mul0 b_mul1 b_step2 b_mul2 b_red2 b_step4 b_mul3 b_red3 b_mul4 b_red4 b_mul5
            b_red5 b_step8 b_mul6 b_mul7 b_red6 b_red7 b_mul8 b_red8 b_kv0 b_kv1 b_kv2 b_ktok16
            b_kv3 b_kv4 b_kv5 b_kv6 b_kv7 b_ktok32 b_kv8 b_kv9 b_rstep16 b_kv10 b_kv11 b_ktok64
            b_rstep32 b_kv12 b_kv13 b_rstep64 b_kv14 b_o0 b_o1 b_cen0 b_cen1 b_var0
            b_var1 b_root b_nrm0 b_nrm1 b_gate b_gn b_wo0 b_wo1 b_xhat20 b_xhat21 b_norm2 b_out0
            b_out1""".split()),
    gpsimd=dict(
        main="""
            b_prod0 b_prod1 f_stats b_prod2 b_s0bd b_prod3 f_sx b_prod4 b_prod5 b_prod6 b_prod7
            f_mix0 b_prod8 b_add1 b_add2 b_add3 b_add4 b_add5 b_add6 b_add7 b_add8 f_mix1 f_mix2
            f_mix3 b_wo0 b_wo1 f_mix4""".split(),
        last="""
            b_prod0 b_prod1 b_prod2 b_prod3 b_prod4 b_prod5 b_prod6 b_prod7 b_prod8 b_s0bd b_add1
            b_add2 b_add3 b_add4 b_add5 b_add6 b_add7 b_add8 b_wo0 b_wo1""".split()),
    scalar=dict(
        main="""
            f_norm b_g f_lora f_mix0 b_vtok f_mix1 f_dec1 b_ktok16 b_ktok32 f_dec2 f_mix2 b_ktok64
            b_ktok128 b_sq0 b_sq1 f_k f_mix3 b_gn f_v b_norm2 f_mix4 b_fk f_r b_fr""".split(),
        last="""
            b_vtok b_ktok16 b_ktok32 b_ktok64 b_ktok128 b_sq0 b_sq1 b_g b_gn b_norm2 b_fk b_fr""".split()),
)


def spread(ap, axis, n):
    shape = list(ap.shape)
    shape[axis] = n
    return ap.broadcast_to(shape)


def wkv_kernel(nc, x, cols, s0, w1, w2a, w2b, dw1, dw2, wk, wv, wr, wg, wo, fk, fr, fv, ident, headmask, tokmask, out):
    with ExitStack() as ctx:
        def sb(name, shape):
            return ctx.enter_context(nc.sbuf_tensor(name, shape, F32))

        def sem(name):
            return ctx.enter_context(nc.semaphore(name))

        cols_s = sb("cols_s", [P, C, NCOLS])
        s0_s = sb("s0_s", [P, B, C, S])
        ident_s = sb("ident_s", [P, P])
        hm_s = sb("hm_s", [P, P])
        tm_s = sb("tm_s", [P, 7])
        u_s = sb("u_s", [P, C, P])
        w1_s = sb("w1_s", [P, C, NMIX * LORA])
        w2a_s = sb("w2a_s", [P, E])
        w2b_s = sb("w2b_s", [LORA, E])
        dw1_s = sb("dw1_s", [P, C, DEC])
        dw2_s = sb("dw2_s", [DEC, E])
        big = {n: sb(n + "_s", [P, C, E]) for n in ("wk", "wv", "wr", "wg", "wo", "fk", "fr", "fv")}
        pause = sb("pause", [P, 1])
        warm = sb("warm", [P, 1])
        eps_s = sb("eps_s", [P, T * H])
        half_s = sb("half_s", [P, T * H])

        xt = sb("xt", [P, 2, T, E])
        st1 = sb("st1", [P, T, 6])
        mv1 = sb("mv1", [P, T, 2])
        ve1 = sb("ve1", [P, T])
        rs1 = sb("rs1", [P, T])
        xhat = sb("xhat", [P, T, E])
        xnT = sb("xnT", [P, C, L + 1])
        sx = sb("sx", [P, C, L])
        xmix = sb("xmix", [P, 3, C, L])
        thA = sb("thA", [P, L])
        thB = sb("thB", [LORA, L])
        dech = sb("dech", [DEC, L])
        rT, kT, vT, wT, gT = (sb(n, [P, 2, C * L]) for n in ("rT", "kT", "vT", "wT", "gT"))

        pp = sb("pp", [P, 3, 1024])
        acc = sb("acc", [P, C * L])
        tot = sb("tot", [P, 1024])
        vtok = sb("vtok", [P, T, E])
        kexp = sb("kexp", [P, 4, T, E])
        sring = sb("sring", [P, 4, 512])
        s0bd = sb("s0bd", [P, C, HP, S])
        gsum = sb("gsum", [P, T * H])
        gvar = sb("gvar", [P, T * H])
        gve = sb("gve", [P, T * H])
        grs = sb("grs", [P, T * H])
        cen = vtok
        x1 = tot[:, :].rearrange("p (t e) -> p t e", t=T)
        st2 = sb("st2", [P, T, 6])
        mv2 = sb("mv2", [P, T, 2])
        ve2 = sb("ve2", [P, T])
        rs2 = sb("rs2", [P, T])
        xn2T = sring[:, :, :].rearrange("p q k -> p (q k)")[:, 0:C * (L + 1)].rearrange("p (c l) -> p c l", c=C)
        adds = sring[:, :, :].rearrange("p q k -> p (q k)")
        xhat2 = cen
        xk = kexp[:, 0, :, :].rearrange("p t e -> p (t e)").rearrange("p (c l) -> p c l", c=C)
        xr = kexp[:, 1, :, :].rearrange("p t e -> p (t e)").rearrange("p (c l) -> p c l", c=C)
        kk = xk
        rr = kexp[:, 2, :, :]
        sq = rr
        yb = kexp[:, 3, :, :].rearrange("p t e -> p (t e)").rearrange("p (c l) -> p c l", c=C)
        sx2 = yb
        outt = kexp[:, 3, :, :]

        FA, FB, BA, BB = (ctx.enter_context(nc.psum_tensor(n, [P, 1024], F32)) for n in ("FA", "FB", "BA", "BB"))

        c_loaded = sem("c_loaded")
        w_loaded = {n: sem(n + "_loaded") for n in
                    ("s0", "w1", "w2", "dw", "wk", "wv", "wr", "wg", "wo", "fk", "fr", "fv")}
        x_loaded = [sem("x_loaded0"), sem("x_loaded1")]
        half_ready = sem("half_ready")
        u_ready = sem("u_ready")
        names = (
            "st1_ready mv1_ready ve1_ready rs1_ready xhat_ready xhatT_ready xnT_ready sx_ready xin_ready lora_ready "
            "th_ready m2_ready mixe_ready mixm_ready mix_ready dech_ready dec1_ready dec2_ready wexp_ready w_ready "
            "k_ready v_ready r_ready gate_ready g_ready projk_ready projv_ready projr_ready projg_ready "
            "p_ready score_ready q_ready qs_ready acc_ready step_ready vtokT_ready vtok_ready ktokT_ready ktok_ready "
            "kv_ready s_ready s128_ready rstep_ready applied s0bd_ready o_ready att_ready attT_ready gsum_ready cen_ready sq_ready gvar_ready "
            "root_ready nrm_ready nrmT_ready y1_ready y_ready wo_ready x1_ready st2_ready mv2_ready ve2_ready "
            "rs2_ready xhat2_ready xhat2T_ready xn2T_ready sx2_ready xk_ready xr_ready fr_ready rr_ready fk_ready "
            "relu_ready kk_ready fv_ready mul_ready out_ready stored").split()
        s_ = {n: sem(n) for n in names}

        def blocks(ap, m):
            return ap.rearrange("p (n two m) -> p n two m", two=2, m=m)

        def totals(m):
            at = sum(C * L // q for q in (2, 4, 8, 16, 32, 64, 128) if q < m)
            return tot[:, at:at + C * L // m]

        def added(i):
            at = [0]
            for m, _, n in DIRECT[1:]:
                at.append(at[-1] + n * L // 2)
            return adds[:, at[i - 1]:at[i]]

        def product(i, par):
            return wT[:, par, :] if i % 2 == 0 else kexp[:, 3, :, :].rearrange("p t e -> p (t e)")

        block = ctx.enter_context(nc.Block())

        def walk(eng, steps, order):
            def run(front, back, order=order["main"]):
                for name in order:
                    which = {"f": front, "b": back}.get(name[0], front or back)
                    if which is not None:
                        steps[name](*which)
            run((0, 0, 0), None, order.get("first", order["main"]))
            run((1, 1, 0), (0, 0, 0))
            with eng.Fori(0, PAIRS) as j:
                run((2 * j + 2, 0, j + 1), (2 * j + 1, 1, j))
                run((2 * j + 3, 1, j + 1), (2 * j + 2, 0, j + 1))
            run(None, (B - 1, 1, B // 2 - 1), order["last"])

        def last(b):
            return isinstance(b, int) and b == B - 1

        def first(b):
            return isinstance(b, int) and b == 0

        slot_read = (("projr_ready", 1), ("projg_ready", 1), ("lora_ready", 0), ("dec1_ready", 0), ("projk_ready", 0))

        @block.sync
        def _(sp):
            def load_x(b, par):
                sp.dma_start(xt[:, par], x[b].rearrange("(t p) e -> p t e", p=P)).then_inc(x_loaded[par], 16)

            load_x(0, 0)
            for dst, src in ((cols_s, cols), (ident_s, ident), (hm_s, headmask), (tm_s, tokmask)):
                sp.dma_start(dst[:], src).then_inc(c_loaded, 16)
            sp.dma_start(w1_s[:], w1).then_inc(w_loaded["w1"], 16)
            sp.dma_start(w2a_s[:], w2a).then_inc(w_loaded["w2"], 16)
            sp.dma_start(w2b_s[:], w2b).then_inc(w_loaded["w2"], 16)
            sp.dma_start(dw1_s[:], dw1).then_inc(w_loaded["dw"], 16)
            sp.dma_start(dw2_s[:], dw2).then_inc(w_loaded["dw"], 16)
            load_x(1, 1)
            sp.dma_start(s0_s[:], s0).then_inc(w_loaded["s0"], 16)
            for n, src in (("wk", wk), ("wv", wv), ("wr", wr), ("wg", wg), ("wo", wo), ("fr", fr), ("fk", fk),
                           ("fv", fv)):
                sp.dma_start(big[n][:], src).then_inc(w_loaded[n], 16)

            def store(b):
                sp.wait_ge(s_["out_ready"], T * b + T)
                sp.dma_start(out[b].rearrange("(t p) e -> p t e", p=P), outt).then_inc(s_["stored"], 16)

            def reload(b, par):
                sp.wait_ge(s_["x1_ready"], T * (b - 1))
                load_x(b, par)

            reload(2, 0)
            store(0)
            with sp.Fori(0, PAIRS - 1) as j:
                reload(2 * j + 3, 1)
                store(2 * j + 1)
                reload(2 * j + 4, 0)
                store(2 * j + 2)
            reload(B - 1, 1)
            store(B - 3)
            store(B - 2)
            store(B - 1)
            sp.wait_ge(s_["stored"], 16 * B)

        @block.gpsimd
        def _(pool):
            nc.gpsimd.memset(half_s[:], -0.5).then_inc(half_ready, 1)
            nc.gpsimd.memset(eps_s[:], EPS).then_inc(half_ready, 1)
            pool.wait_ge(half_ready, 2)

            def inverse_root(mv_ready, mv, ve, ve_ready, rs, rs_ready, b):
                pool.wait_ge(mv_ready, b + 1)
                nc.gpsimd.tensor_tensor(ve, mv, eps_s[:, 0:ve.shape[1]], ALU.add).then_inc(ve_ready, 1)
                pool.wait_ge(ve_ready, b + 1)
                nc.gpsimd.tensor_tensor(rs, ve, half_s[:, 0:ve.shape[1]], ALU.pow).then_inc(rs_ready, 1)

            def f_stats(b, par, n):
                inverse_root(s_["mv1_ready"], mv1[:, :, 1], ve1[:], s_["ve1_ready"], rs1[:], s_["rs1_ready"], b)

            def f_sx(b, par, n):
                if first(b):
                    pool.wait_ge(c_loaded, 16 * 4)
                    for c in range(C):
                        nc.gpsimd.tensor_tensor(u_s[:, c, :], hm_s[:], spread(cols_s[:, c, FAAAA:FAAAA + 1], 1, P),
                                                ALU.mult).then_inc(u_ready, 1)
                    return
                pool.wait_ge(s_["xnT_ready"], b + 1)
                pool.wait_ge(s_["mixm_ready"], NMIX * b)
                nc.gpsimd.tensor_tensor(sx[:], xnT[:, :, 0:L], xnT[:, :, 1:L + 1],
                                        ALU.subtract).then_inc(s_["sx_ready"], 1)

            def f_mix(j):
                def run(b, par, n):
                    if first(b):
                        return
                    pool.wait_ge(s_["mixe_ready"], NMIX * b + j + 1)
                    slot = xmix[:, j % 3]
                    nc.gpsimd.tensor_tensor(slot, slot, sx[:], ALU.mult).then_inc(s_["mixm_ready"], 1)
                    pool.wait_ge(s_["mixm_ready"], NMIX * b + j + 1)
                    nc.gpsimd.tensor_tensor(slot, slot, xnT[:, :, 1:L + 1], ALU.add).then_inc(s_["mix_ready"], 1)
                return run

            def b_prod(i):
                m, c0, nc_ = DIRECT[i]

                def run(b, par, n):
                    r, k = rT[:, par, c0 * L:(c0 + nc_) * L], kT[:, par, c0 * L:(c0 + nc_) * L]
                    if m == 0:
                        pool.wait_ge(s_["r_ready"], b + 1)
                        pool.wait_ge(s_["k_ready"], b + 1)
                    elif m > 1 and c0 == 0:
                        pool.wait_ge(s_["step_ready"], 7 * b + {2: 1, 4: 2, 8: 3}[m])
                    if i >= 3 or not first(b):
                        pool.wait_ge(s_["score_ready"], ND * b + i - 2)
                    slot = pp[:, i % 3, :]
                    if m == 0:
                        ins = nc.gpsimd.tensor_tensor(slot, r, k, ALU.mult)
                    elif m == 1:
                        ins = nc.gpsimd.tensor_tensor(slot[:, 0:C * L // 2], blocks(r, 1)[:, :, 1, 0],
                                                      blocks(k, 1)[:, :, 0, 0], ALU.mult)
                    else:
                        ins = nc.gpsimd.tensor_tensor(
                            slot.rearrange("p (n i j) -> p n i j", i=m, j=m),
                            spread(blocks(r, m)[:, :, 1, :].unsqueeze(3), 3, m),
                            spread(blocks(k, m)[:, :, 0, :].unsqueeze(2), 2, m), ALU.mult)
                    ins.then_inc(s_["p_ready"], 1)
                return run

            def b_add(i):
                m, c0, nc_ = DIRECT[i]

                def run(b, par, n):
                    if m == 1:
                        pool.wait_ge(s_["q_ready"], ND * b + i + 1)
                    else:
                        pool.wait_ge(s_["qs_ready"], (ND - 2) * b + i - 1)
                    if i > 1:
                        pool.wait_ge(s_["acc_ready"], (ND - 1) * b + i - 1)
                    a = blocks(acc[:, c0 * L:(c0 + nc_) * L], m)[:, :, 1, :]
                    nc.gpsimd.tensor_tensor(a, a, added(i).rearrange("p (n m) -> p n m", m=m),
                                            ALU.add).then_inc(s_["acc_ready"], 1)
                return run

            def b_s0bd(b, par, n):
                pool.wait_ge(w_loaded["s0"], 16)
                if not first(b):
                    pool.wait_ge(s_["o_ready"], b)
                    pool.wait_ge(s_["s_ready"], NS * b)
                nc.gpsimd.tensor_tensor(
                    s0bd[:], spread(s0_s[:, b, :, :].unsqueeze(2), 2, HP),
                    spread(hm_s[:, :].rearrange("p (h s) -> p h s", h=HP).unsqueeze(1), 1, C),
                    ALU.mult).then_inc(s_["s0bd_ready"], 1)

            def b_wo(t):
                def run(b, par, n):
                    inverse_root(s_["mv2_ready"], mv2[:, t:t + 1, 1], ve2[:, t:t + 1], s_["ve2_ready"],
                                 rs2[:, t:t + 1], s_["rs2_ready"], T * b + t)
                return run

            steps = dict(f_stats=f_stats, f_sx=f_sx, b_s0bd=b_s0bd)
            steps.update({f"b_wo{t}": b_wo(t) for t in range(T)})
            steps.update({f"b_add{i}": b_add(i) for i in range(1, ND)})
            steps.update({f"f_mix{j}": f_mix(j) for j in range(NMIX)})
            steps.update({f"b_prod{i}": b_prod(i) for i in range(ND)})
            walk(pool, steps, ORDER["gpsimd"])

        @block.tensor
        def _(pe):
            def transpose_tokens(dst, src, tiles=range(T)):
                for t in tiles:
                    for c in range(C):
                        ins = nc.tensor.transpose(dst[:, t * E + c * P:t * E + (c + 1) * P],
                                                  src[:, c * L + t * P:c * L + (t + 1) * P], ident_s[:])
                return ins

            def transpose_channels(dst, src, tiles=range(T)):
                for t in tiles:
                    for c in range(C):
                        ins = nc.tensor.transpose(dst[:, c * L + t * P:c * L + (t + 1) * P],
                                                  src[:, t, c * P:(c + 1) * P], ident_s[:])
                return ins

            def project(dst, weight, src, tiles=range(C)):
                for c in tiles:
                    for q in range(C):
                        ins = nc.tensor.matmul(dst[:, c * L:(c + 1) * L], weight[:, q, c * P:(c + 1) * P],
                                               src[:, q, :], start=(q == 0), stop=(q == C - 1))
                return ins

            def project_tokens(dst, weight, src, tiles=range(T)):
                for t in tiles:
                    for q in range(C):
                        ins = nc.tensor.matmul(dst[:, t * E:(t + 1) * E], src[:, q, t * P:(t + 1) * P],
                                               weight[:, q, :], start=(q == 0), stop=(q == C - 1))
                return ins

            def loaded(name, n=16):
                pe.wait_ge(w_loaded[name], n)

            def f_norm(b, par, n):
                if first(b):
                    pe.wait_ge(c_loaded, 16 * 4)
                pe.wait_ge(s_["xhat_ready"], b + 1)
                if not first(b):
                    pe.wait_ge(s_["mixe_ready"], NMIX * b)
                    pe.wait_ge(s_["out_ready"], T * (b - 1))
                transpose_channels(FA, xhat).then_inc(s_["xhatT_ready"], 1)

            def f_lora(b, par, n):
                loaded("w1")
                pe.wait_ge(s_["xin_ready"], b + 1)
                if not first(b):
                    pe.wait_ge(s_["g_ready"], b)
                    pe.wait_ge(s_["gate_ready"], b)
                for q in range(C):
                    nc.tensor.matmul(FB[:, 0:L], w1_s[:, q, 0:P], xmix[:, 2, q, :], start=(q == 0), stop=(q == C - 1))
                for q in range(C):
                    ins = nc.tensor.matmul(FB[0:LORA, 512:512 + L], w1_s[:, q, P:P + LORA], xmix[:, 2, q, :],
                                           start=(q == 0), stop=(q == C - 1))
                ins.then_inc(s_["lora_ready"], 1)

            def f_m2(j):
                i = MIXES[j]

                def run(b, par, n):
                    if j == 0:
                        loaded("w2", 32)
                        pe.wait_ge(s_["th_ready"], 2 * b + 2)
                    else:
                        pe.wait_ge(s_["mixe_ready"], NMIX * b + j)
                    for c in range(C):
                        if i < 4:
                            lhs, rhs = w2a_s[32 * i:32 * i + 32, c * P:(c + 1) * P], thA[32 * i:32 * i + 32, :]
                        else:
                            lhs, rhs = w2b_s[:, c * P:(c + 1) * P], thB[:, :]
                        ins = nc.tensor.matmul(FA[:, c * L:(c + 1) * L], lhs, rhs, start=True, stop=True)
                    ins.then_inc(s_["m2_ready"], 1)
                return run

            def f_dec1(b, par, n):
                loaded("dw", 32)
                pe.wait_ge(s_["mix_ready"], NMIX * b + 1)
                pe.wait_ge(s_["th_ready"], 2 * b + 2)
                if not first(b):
                    pe.wait_ge(s_["vtok_ready"], b)
                for q in range(C):
                    ins = nc.tensor.matmul(FB[0:DEC, 0:L], dw1_s[:, q, :], xmix[:, 0, q, :],
                                           start=(q == 0), stop=(q == C - 1))
                ins.then_inc(s_["dec1_ready"], 1)

            def f_dec2(b, par, n):
                pe.wait_ge(s_["dech_ready"], b + 1)
                if not first(b):
                    pe.wait_ge(s_["ktok_ready"], 4 * b - 3)
                for c in range(C):
                    ins = nc.tensor.matmul(FB[:, c * L:(c + 1) * L], dw2_s[:, c * P:(c + 1) * P], dech[:],
                                           start=True, stop=True)
                ins.then_inc(s_["dec2_ready"], 1)

            def proj(read, j, weight, done, c):
                def run(b, par, n):
                    if c == 0:
                        loaded(weight)
                        pe.wait_ge(s_["mix_ready"], NMIX * b + j + 1)
                        pe.wait_ge(s_[read], b + 1)
                    ins = project(FB, big[weight], xmix[:, j % 3], [c])
                    if c == C - 1:
                        ins.then_inc(s_[done], 1)
                return run

            def b_g(c):
                def run(b, par, n):
                    if last(b):
                        pe.wait_ge(s_["ktok_ready"], 4 * b + 1)
                    proj("r_ready", 4, "wg", "projg_ready", c)(b, par, n)
                return run

            def b_score(i):
                m, c0, nc_ = DIRECT[i]
                dst = BA if i % 2 == 0 else BB

                def run(b, par, n):
                    pe.wait_ge(s_["p_ready"], ND * b + i + 1)
                    if i == 0:
                        pe.wait_ge(u_ready, C)
                        pe.wait_ge(s_["rr_ready"], b)
                    elif i == 1:
                        if not first(b):
                            pe.wait_ge(s_["relu_ready"], b)
                    else:
                        pe.wait_ge(s_["q_ready"], ND * b + i - 1)
                    slot = pp[:, i % 3, :]
                    if m == 0:
                        for c in range(C):
                            ins = nc.tensor.matmul(dst[:, c * L:(c + 1) * L], u_s[:, c, :], slot[:, c * L:(c + 1) * L],
                                                   start=True, stop=True)
                    else:
                        for h in range(1 if m == 1 else 2):
                            ins = nc.tensor.matmul(dst[:, h * 512:(h + 1) * 512], hm_s[:],
                                                   slot[:, h * 512:(h + 1) * 512], start=True, stop=True)
                    ins.then_inc(s_["score_ready"], 1)
                return run

            def b_vtok(b, par, n):
                pe.wait_ge(s_["v_ready"], b + 1)
                if not last(b):
                    pe.wait_ge(s_["th_ready"], 2 * b + 4)
                else:
                    pe.wait_ge(s_["r_ready"], b + 1)
                transpose_tokens(FB, vT[:, par, :]).then_inc(s_["vtokT_ready"], 1)

            def b_ktok(l):
                m = LEVELS[l]

                def run(b, par, n):
                    pe.wait_ge(s_["step_ready"], 7 * b + (4, 5, 6, 7)[l])
                    if l == 0:
                        pe.wait_ge(s_["vtok_ready"], b + 1)
                        if not last(b):
                            pe.wait_ge(s_["dech_ready"], b + 2)
                    else:
                        pe.wait_ge(s_["s_ready"], NS * b + LEVEL_AT[m])
                    src = kT[:, par, :]
                    if m < P:
                        ins = transpose_tokens(BA if l else FB, src)
                    else:
                        for c in range(C):
                            ins = nc.tensor.transpose(BA[:, c * P:(c + 1) * P], src[:, c * L:c * L + P], ident_s[:])
                    ins.then_inc(s_["ktokT_ready"], 1)
                return run

            def b_kv(q):
                m, pairs = STATE[q]
                bank, per = BA[:, q % 2 * 512:], max(P // (2 * m), 1)

                def run(b, par, n):
                    pe.wait_ge(s_["ktok_ready"], 4 * b + LEVELS.index(m) + 1)
                    if q < 2:
                        pe.wait_ge(s_["q_ready"], ND * b + ND)
                    if q >= LEVEL_AT[m] + 2:
                        pe.wait_ge(s_["s_ready"], NS * b + q - 1)
                    for j, (c, i) in enumerate(pairs):
                        ins = nc.tensor.matmul(bank[:, j * P:(j + 1) * P],
                                               kexp[:, KEYS_AT[m] + i % per, i // per, c * P:(c + 1) * P],
                                               vtok[:, i // per, c * P:(c + 1) * P], start=True, stop=True)
                    ins.then_inc(s_["kv_ready"], 1)
                return run

            def b_apply(q):
                m, pairs = STATE[q]

                def run(b, par, n):
                    if q == 0:
                        pe.wait_ge(s_["step_ready"], 7 * b + 4)
                    elif q == LEVEL_AT[m]:
                        pe.wait_ge(s_["rstep_ready"], 3 * b + LEVELS.index(m))
                    pe.wait_ge(s_["s_ready"], NS * b + q + 1)
                    for j, (c, i) in enumerate(pairs):
                        t0 = 2 * m * i + m
                        ins = nc.tensor.matmul(BB[:, c * L + t0:c * L + t0 + m], sring[:, q % 4, j * P:(j + 1) * P],
                                               rT[:, par, c * L + t0:c * L + t0 + m],
                                               start=(m == LEVELS[0] and c % 2 == 0 and i == 0), stop=False,
                                               skip_group_check=True)
                    ins.then_inc(s_["applied"], 1)
                return run

            def b_s0(b, par, n):
                pe.wait_ge(s_["rstep_ready"], 3 * b + 3)
                pe.wait_ge(s_["s0bd_ready"], b + 1)
                for c in range(C):
                    ins = nc.tensor.matmul(BB[:, c * L:c * L + P],
                                           s0bd[:, c, :, :].rearrange("p h s -> p (h s)"),
                                           rT[:, par, c * L:c * L + P], start=False, stop=True,
                                           skip_group_check=True)
                ins.then_inc(s_["o_ready"], 1)

            def b_att(t):
                def run(b, par, n):
                    pe.wait_ge(s_["att_ready"], T * b + t + 1)
                    pe.wait_ge(s_["s_ready"], NS * b + NS)
                    transpose_tokens(BA, acc[:, :], [t]).then_inc(s_["attT_ready"], 1)
                return run

            def b_gn(t):
                def run(b, par, n):
                    pe.wait_ge(s_["nrm_ready"], T * b + t + 1)
                    transpose_channels(BA, cen, [t]).then_inc(s_["nrmT_ready"], 1)
                return run

            def b_wo(t):
                def run(b, par, n):
                    loaded("wo")
                    pe.wait_ge(s_["y_ready"], b + 1)
                    project_tokens(BA, big["wo"], yb, [t]).then_inc(s_["wo_ready"], 1)
                return run

            def b_norm2(t):
                def run(b, par, n):
                    pe.wait_ge(s_["xhat2_ready"], T * b + t + 1)
                    transpose_channels(BA, xhat2, [t]).then_inc(s_["xhat2T_ready"], 1)
                return run

            def b_fk(b, par, n):
                loaded("fk")
                pe.wait_ge(s_["xk_ready"], b + 1)
                project(BB, big["fk"], xk).then_inc(s_["fk_ready"], 1)

            def b_fr(b, par, n):
                loaded("fr")
                pe.wait_ge(s_["xr_ready"], b + 1)
                project_tokens(BA, big["fr"], xr).then_inc(s_["fr_ready"], 1)

            def b_fv(t):
                def run(b, par, n):
                    loaded("fv")
                    pe.wait_ge(s_["kk_ready"], b + 1)
                    if not last(b):
                        pe.wait_ge(s_["mixe_ready"], NMIX * (b + 2))
                    project_tokens(FA, big["fv"], kk, [t]).then_inc(s_["fv_ready"], 1)
                return run

            def warm(n):
                def run(b, par, _):
                    pe.wait_ge(c_loaded, 16 * 4)
                    for _ in range(n):
                        nc.tensor.matmul((BB if first(b) else FA)[:, 0:P], ident_s[:], hm_s[:], start=True, stop=True)
                return run

            steps = dict(f_norm=f_norm, f_lora=f_lora, f_dec1=f_dec1, f_dec2=f_dec2,
                         b_vtok=b_vtok, b_s0=b_s0, b_fk=b_fk, b_fr=b_fr)
            steps.update({name: warm(int(name[4:])) for name in ORDER["tensor"]["first"] + ORDER["tensor"]["last"]
                          if name[:4] == "warm"})
            for t in range(T):
                steps.update({f"b_att{t}": b_att(t), f"b_gn{t}": b_gn(t), f"b_wo{t}": b_wo(t),
                              f"b_norm2{t}": b_norm2(t), f"b_fv{t}": b_fv(t)})
            steps.update({f"f_m2{j}": f_m2(j) for j in range(NMIX)})
            for c in range(C):
                steps[f"f_k{c}"] = proj("wexp_ready", 1, "wk", "projk_ready", c)
                steps[f"f_v{c}"] = proj("k_ready", 2, "wv", "projv_ready", c)
                steps[f"f_r{c}"] = proj("v_ready", 3, "wr", "projr_ready", c)
                steps[f"b_g{c}"] = b_g(c)
            steps.update({f"b_score{i}": b_score(i) for i in range(ND)})
            steps.update({f"b_ktok{m}": b_ktok(l) for l, m in enumerate(LEVELS)})
            steps.update({f"b_kv{q}": b_kv(q) for q in range(NS)})
            steps.update({f"b_apply{q}": b_apply(q) for q in range(NS)})
            walk(pe, steps, ORDER["tensor"])

        @block.scalar
        def _(act):
            def col(i):
                return lambda c: cols_s[:, c, i:i + 1]

            def f_norm(b, par, n):
                if first(b):
                    act.wait_ge(half_ready, 2)
                    nc.scalar.activation(warm[:], eps_s[:, 0:1], ACT.Identity)
                    act.wait_ge(c_loaded, 16 * 4)
                else:
                    act.wait_ge(s_["mix_ready"], NMIX * b)
                act.wait_ge(s_["xhatT_ready"], b + 1)
                nc.scalar.activation(xnT[:, :, 0:1], cols_s[:, :, bass.ds(PREV_ATT + b, 1)], ACT.Copy)
                for c in range(C):
                    ins = nc.scalar.activation(xnT[:, c, 1:L + 1], FA[:, c * L:(c + 1) * L], ACT.Identity,
                                               bias=col(LN1_B)(c), scale=col(LN1_W)(c))
                ins.then_inc(s_["xnT_ready"], 1)

            def f_lora(b, par, n):
                act.wait_ge(s_["lora_ready"], b + 1)
                if not first(b):
                    act.wait_ge(s_["m2_ready"], NMIX * b)
                nc.scalar.activation(thA[:], FB[:, 0:L], ACT.Tanh).then_inc(s_["th_ready"], 1)
                ins = nc.scalar.activation(thB[:], FB[0:LORA, 512:512 + L], ACT.Tanh)
                ins.then_inc(s_["th_ready"], 1)

            def f_dec1(b, par, n):
                act.wait_ge(s_["dec1_ready"], b + 1)
                nc.scalar.activation(dech[:], FB[0:DEC, 0:L], ACT.Tanh).then_inc(s_["dech_ready"], 1)

            def f_dec2(b, par, n):
                act.wait_ge(s_["dec2_ready"], b + 1)
                if not first(b):
                    act.wait_ge(s_["o_ready"], b - 1)
                for c in range(C):
                    ins = nc.scalar.activation(wT[:, par, c * L:(c + 1) * L], FB[:, c * L:(c + 1) * L], ACT.Exp,
                                               bias=col(TIME_DECAY)(c))
                ins.then_inc(s_["wexp_ready"], 1)
                act.wait_ge(s_["wexp_ready"], b + 1)
                nc.scalar.activation(wT[:, par, :], wT[:, par, :], ACT.Exp, scale=-1.0).then_inc(s_["w_ready"], 1)

            def f_proj(done, dst, ready):
                def run(b, par, n):
                    act.wait_ge(s_[done], b + 1)
                    if not first(b):
                        act.wait_ge(s_["o_ready"], b - 1)
                    nc.scalar.copy(dst[:, par, :], FB[:]).then_inc(s_[ready], 1)
                return run

            def f_mix(j):
                def run(b, par, n):
                    if first(b):
                        return
                    act.wait_ge(s_["m2_ready"], NMIX * b + j + 1)
                    used, behind = slot_read[j]
                    if not (first(b) and behind):
                        act.wait_ge(s_[used], b + 1 - behind)
                    for c in range(C):
                        ins = nc.scalar.activation(xmix[:, j % 3, c, :], FA[:, c * L:(c + 1) * L], ACT.Identity,
                                                   bias=col(MAA_STACK + MIXES[j])(c))
                    ins.then_inc(s_["mixe_ready"], 1)
                return run

            def b_g(b, par, n):
                act.wait_ge(s_["projg_ready"], b + 1)
                nc.scalar.activation(gT[:, par, :], FB[:], ACT.Tanh, scale=0.5).then_inc(s_["gate_ready"], 1)

            def b_vtok(b, par, n):
                act.wait_ge(s_["vtokT_ready"], b + 1)
                nc.scalar.copy(vtok[:, :, :].rearrange("p t e -> p (t e)"), FB[:]).then_inc(s_["vtok_ready"], 1)

            def b_ktok(l):
                m = LEVELS[l]

                def run(b, par, n):
                    act.wait_ge(s_["ktokT_ready"], 4 * b + l + 1)
                    if l:
                        act.wait_ge(s_["kv_ready"], NS * b + LEVEL_AT[LEVELS[1]])
                    if m < P:
                        at = {16: 0, 32: 4, 64: 6}[m]
                        for i in range(P // (2 * m)):
                            if KEYS_AT[m] + i == 3:
                                act.wait_ge(s_["qs_ready"], (ND - 2) * b + LAST_ODD - 1)
                            ins = nc.scalar.activation(kexp[:, KEYS_AT[m] + i, :, :].rearrange("p t e -> p (t e)"),
                                                       (BA if l else FB)[:],
                                                       ACT.Copy, scale=tm_s[:, at + i:at + i + 1])
                    else:
                        ins = nc.scalar.copy(kexp[:, KEYS_AT[m], 0, :], BA[:, 0:E])
                    ins.then_inc(s_["ktok_ready"], 1)
                return run

            def b_sq(t):
                def run(b, par, n):
                    act.wait_ge(s_["cen_ready"], T * b + t + 1)
                    nc.scalar.activation(sq[:, t, :], cen[:, t, :], ACT.Square,
                                         scale=S ** -0.5).then_inc(s_["sq_ready"], 1)
                return run

            def b_gn(b, par, n):
                act.wait_ge(s_["nrmT_ready"], T * b + T)
                for c in range(C):
                    ins = nc.scalar.activation(yb[:, c, :], BA[:, c * L:(c + 1) * L], ACT.Identity,
                                               bias=col(GN_B)(c), scale=col(GN_W)(c))
                ins.then_inc(s_["y1_ready"], 1)

            def b_norm2(b, par, n):
                act.wait_ge(s_["xhat2T_ready"], T * b + T)
                nc.scalar.activation(xn2T[:, :, 0:1], cols_s[:, :, bass.ds(PREV_FFN + b, 1)], ACT.Copy)
                for c in range(C):
                    ins = nc.scalar.activation(xn2T[:, c, 1:L + 1], BA[:, c * L:(c + 1) * L], ACT.Identity,
                                               bias=col(LN2_B)(c), scale=col(LN2_W)(c))
                ins.then_inc(s_["xn2T_ready"], 1)

            def b_fk(b, par, n):
                act.wait_ge(s_["fk_ready"], b + 1)
                kf = kk.rearrange("p c l -> p (c l)")
                nc.scalar.activation(kf, BB[:], ACT.Relu).then_inc(s_["relu_ready"], 1)
                act.wait_ge(s_["relu_ready"], b + 1)
                nc.scalar.activation(kf, kf, ACT.Square).then_inc(s_["kk_ready"], 1)

            def b_fr(b, par, n):
                act.wait_ge(s_["fr_ready"], b + 1)
                nc.scalar.activation(rr.rearrange("p t e -> p (t e)"), BA[:], ACT.Tanh,
                                     scale=0.5).then_inc(s_["rr_ready"], 1)

            steps = dict(f_norm=f_norm, f_lora=f_lora, f_dec1=f_dec1, f_dec2=f_dec2,
                         f_k=f_proj("projk_ready", kT, "k_ready"), f_v=f_proj("projv_ready", vT, "v_ready"),
                         f_r=f_proj("projr_ready", rT, "r_ready"), b_g=b_g,
                         b_vtok=b_vtok, b_sq0=b_sq(0), b_sq1=b_sq(1), b_gn=b_gn, b_norm2=b_norm2, b_fk=b_fk,
                         b_fr=b_fr)
            steps.update({f"f_mix{j}": f_mix(j) for j in range(NMIX)})
            steps.update({f"b_ktok{m}": b_ktok(l) for l, m in enumerate(LEVELS)})
            walk(act, steps, ORDER["scalar"])

        @block.vector
        def _(dve):
            def stats(src, st, st_ready, mv, mv_ready, b, tiles=range(T)):
                for t in tiles:
                    ins = nc.vector.bn_stats(st[:, t, :], src[:, t, :])
                ins.then_inc(st_ready, 1)
                dve.wait_ge(st_ready, b + 1)
                nc.vector.memset(pause[:], 0.0)
                for t in tiles:
                    ins = nc.vector.bn_aggr(mv[:, t, :], st[:, t, :])
                ins.then_inc(mv_ready, 1)

            def norm(dst, src, mv, rs, tiles=range(T)):
                for t in tiles:
                    ins = nc.vector.tensor_scalar(dst[:, t, :], src[:, t, :], mv[:, t, 0:1], rs[:, t:t + 1],
                                                  ALU.subtract, ALU.mult)
                return ins

            def f_stats(b, par, n):
                dve.wait_ge(x_loaded[par], 16 * n + 16)
                stats(xt[:, par], st1, s_["st1_ready"], mv1, s_["mv1_ready"], b)

            def f_norm(b, par, n):
                dve.wait_ge(s_["rs1_ready"], b + 1)
                if not first(b):
                    dve.wait_ge(s_["xhatT_ready"], b)
                norm(xhat, xt[:, par], mv1, rs1).then_inc(s_["xhat_ready"], 1)

            def f_xin(b, par, n):
                if first(b):
                    dve.wait_ge(c_loaded, 16 * 4)
                    dve.wait_ge(s_["xnT_ready"], 1)
                    nc.vector.tensor_tensor(sx[:], xnT[:, :, 0:L], xnT[:, :, 1:L + 1],
                                            ALU.subtract).then_inc(s_["sx_ready"], 1)
                dve.wait_ge(s_["sx_ready"], b + 1)
                if not first(b):
                    dve.wait_ge(s_["projv_ready"], b)
                for c in range(C):
                    ins = nc.vector.scalar_tensor_tensor(out=xmix[:, 2, c, :], in0=sx[:, c, :],
                                                         scalar=cols_s[:, c, MAA_X:MAA_X + 1],
                                                         in1=xnT[:, c, 1:L + 1], op0=ALU.mult, op1=ALU.add)
                ins.then_inc(s_["xin_ready"], 1)

            def f_mix(j):
                def run(b, par, n):
                    if not first(b):
                        return
                    dve.wait_ge(s_["m2_ready"], j + 1)
                    used, behind = slot_read[j]
                    if not behind:
                        dve.wait_ge(s_[used], 1)
                    for c in range(C):
                        ins = nc.vector.scalar_tensor_tensor(out=xmix[:, j % 3, c, :], in0=FA[:, c * L:(c + 1) * L],
                                                             scalar=cols_s[:, c, MAA_STACK + MIXES[j]:MAA_STACK + MIXES[j] + 1],
                                                             in1=sx[:, c, :], op0=ALU.add, op1=ALU.mult)
                    ins.then_inc(s_["mixe_ready"], 1)
                    dve.wait_ge(s_["mixe_ready"], j + 1)
                    for cs, ready in ((slice(0, C // 2), "mixm_ready"), (slice(C // 2, C), "mix_ready")):
                        slot = xmix[:, j % 3, cs, :]
                        nc.vector.tensor_tensor(slot, slot, xnT[:, cs, 1:L + 1], ALU.add).then_inc(s_[ready], 1)
                return run

            def b_gate(b, par, n):
                dve.wait_ge(s_["gate_ready"], b + 1)
                nc.vector.scalar_tensor_tensor(out=gT[:, par, :], in0=gT[:, par, :], scalar=1.0, in1=FB[:],
                                               op0=ALU.add, op1=ALU.mult).then_inc(s_["g_ready"], 1)

            def decay_keys(par, m):
                w = wT[:, par, :] if m == 1 else totals(m)
                k = blocks(kT[:, par, :], m)[:, :, 0, :]
                return nc.vector.tensor_tensor(k, k, spread(blocks(w, 1)[:, :, 1, :], 2, m), ALU.mult)

            def decay_receptances(par, m):
                w = wT[:, par, :] if m == 1 else totals(m)
                r = blocks(rT[:, par, :], m)[:, :, 1, :]
                return nc.vector.tensor_tensor(r, r, spread(blocks(w, 1)[:, :, 0, :], 2, m), ALU.mult)

            def decay_totals(par, m):
                w = wT[:, par, :] if m == 1 else totals(m)
                return nc.vector.tensor_tensor(totals(2 * m), blocks(w, 1)[:, :, 0, 0], blocks(w, 1)[:, :, 1, 0],
                                               ALU.mult)

            def b_step(m):
                last = max(i for i, piece in enumerate(DIRECT) if piece[0] == m)

                def run(b, par, n):
                    dve.wait_ge(s_["p_ready"], ND * b + last + 1)
                    if m == 1:
                        dve.wait_ge(s_["w_ready"], b + 1)
                        if not first(b):
                            dve.wait_ge(s_["out_ready"], T * b)
                    else:
                        dve.wait_ge(s_["step_ready"], 7 * b + m.bit_length() - 1)
                    decay_totals(par, m)
                    decay_keys(par, m)
                    decay_receptances(par, m).then_inc(s_["step_ready"], 1)
                return run

            def b_mul(i):
                m, c0, nc_ = DIRECT[i]
                src = BA if i % 2 == 0 else BB

                def run(b, par, n):
                    if m == 0:
                        dve.wait_ge(s_["v_ready"], b + 1)
                        dve.wait_ge(s_["score_ready"], ND * b + 1)
                        if not first(b):
                            dve.wait_ge(s_["attT_ready"], T * b)
                        nc.vector.tensor_tensor(acc[:], src[:], vT[:, par, :], ALU.mult).then_inc(s_["q_ready"], 1)
                        return
                    v = blocks(vT[:, par, c0 * L:(c0 + nc_) * L], m)[:, :, 0, :]
                    dve.wait_ge(s_["score_ready"], ND * b + i + 1)
                    if m == 1:
                        nc.vector.tensor_tensor(added(i), src[:, 0:512], v.rearrange("p n m -> p (n m)"),
                                                ALU.mult).then_inc(s_["q_ready"], 1)
                        return
                    if i == 2:
                        dve.wait_ge(s_["step_ready"], 7 * b + 1)
                    elif i == 3:
                        if not first(b):
                            dve.wait_ge(s_["stored"], 16 * b)
                    else:
                        dve.wait_ge(s_["qs_ready"], (ND - 2) * b + i - 3)
                    nc.vector.tensor_tensor(product(i, par).rearrange("p (n i j) -> p n i j", i=m, j=m),
                                            src[:].rearrange("p (n i j) -> p n i j", i=m, j=m),
                                            spread(v.unsqueeze(2), 2, m), ALU.mult).then_inc(s_["q_ready"], 1)
                return run

            def b_red(i):
                m = DIRECT[i][0]

                def run(b, par, n):
                    dve.wait_ge(s_["q_ready"], ND * b + i + 1)
                    nc.vector.tensor_reduce(added(i), product(i, par).rearrange("p (n j) -> p n j", j=m), AX.X,
                                            ALU.add).then_inc(s_["qs_ready"], 1)
                return run

            def b_ktok(l):
                m = LEVELS[l]

                def run(b, par, n):
                    if m == P:
                        return
                    dve.wait_ge(s_["step_ready"], 7 * b + 4 + l)
                    dve.wait_ge(s_["ktokT_ready"], 4 * b + l + 1)
                    decay_totals(par, m)
                    decay_keys(par, m).then_inc(s_["step_ready"], 1)
                return run

            def b_kv(q):
                def run(b, par, n):
                    dve.wait_ge(s_["kv_ready"], NS * b + q + 1)
                    if q < 4:
                        dve.wait_ge(s_["acc_ready"], (ND - 1) * b + (1, 2, 4, ND - 1)[q])
                    if q >= 4:
                        dve.wait_ge(s_["applied"], NS * b + q - 3)
                    nc.vector.tensor_tensor(sring[:, q % 4, :].rearrange("p (n k) -> p n k", k=P),
                                            BA[:, q % 2 * 512:q % 2 * 512 + 512].rearrange("p (n k) -> p n k", k=P),
                                            spread(hm_s[:, :].unsqueeze(1), 1, 4),
                                            ALU.mult).then_inc(s_["s128_ready" if STATE[q][0] == P else "s_ready"], 1)
                    if STATE[q][0] == P:
                        dve.wait_ge(s_["s128_ready"], b + 1)
                        dve.wait_ge(s_["s0bd_ready"], b + 1)
                        dve.wait_ge(s_["step_ready"], 7 * b + 7)
                        for c in range(C):
                            state = sring[:, q % 4, c * P:(c + 1) * P]
                            ins = nc.vector.scalar_tensor_tensor(
                                out=state, in0=s0bd[:, c, :, :].rearrange("p h s -> p (h s)"),
                                scalar=totals(P)[:, 2 * c:2 * c + 1], in1=state, op0=ALU.mult, op1=ALU.add)
                        ins.then_inc(s_["s_ready"], 1)
                return run

            def b_rstep(l):
                m = LEVELS[l]
                last = max(q for q in range(NS) if STATE[q][0] == m)

                def run(b, par, n):
                    dve.wait_ge(s_["applied"], NS * b + last + 1)
                    dve.wait_ge(s_["step_ready"], 7 * b + 4 + l)
                    if l:
                        dve.wait_ge(s_["rstep_ready"], 3 * b + l)
                    decay_receptances(par, m).then_inc(s_["rstep_ready"], 1)
                return run

            def b_o(t):
                def run(b, par, n):
                    dve.wait_ge(s_["o_ready"], b + 1)
                    dve.wait_ge(s_["applied"], NS * (b + 1))
                    o, a = (z[:, :].rearrange("p (c l) -> p c l", c=C)[:, :, t * P:(t + 1) * P] for z in (BB, acc))
                    nc.vector.tensor_tensor(a, o, a, ALU.add).then_inc(s_["att_ready"], 1)
                return run

            def heads(ap):
                return ap.rearrange("p (h s) -> p h s", s=S)

            def root(b):
                i32 = mybir.dt.int32
                done = ROOT * b

                def landed(ins, n):
                    ins.then_inc(s_["root_ready"], 1)
                    dve.wait_ge(s_["root_ready"], done + n)

                landed(nc.vector.tensor_scalar(gve[:], gvar[:], EPS, None, ALU.add), 1)
                landed(nc.vector.tensor_scalar(gsum[:].bitcast(i32), gve[:].bitcast(i32), 1, None,
                                               ALU.logical_shift_right), 2)
                landed(nc.vector.tensor_scalar(grs[:].bitcast(i32), gsum[:].bitcast(i32), -1.0,
                                               float(0x5F3759DF), ALU.mult, ALU.add), 3)
                for i in range(4, ROOT, 3):
                    landed(nc.vector.tensor_tensor(gsum[:], grs[:], grs[:], ALU.mult), i)
                    landed(nc.vector.scalar_tensor_tensor(out=gsum[:], in0=gsum[:], scalar=-0.5, in1=gve[:],
                                                          op0=ALU.mult, op1=ALU.mult), i + 1)
                    ins = nc.vector.scalar_tensor_tensor(out=grs[:], in0=gsum[:], scalar=1.5, in1=grs[:],
                                                         op0=ALU.add, op1=ALU.mult)
                    landed(ins, i + 2)

            def b_cen(t):
                hs = slice(t * H, (t + 1) * H)
                bank = BA[:, t * E:(t + 1) * E]

                def run(b, par, n):
                    dve.wait_ge(s_["attT_ready"], T * b + t + 1)
                    nc.vector.tensor_reduce(gsum[:, hs], heads(bank), AX.X, ALU.add).then_inc(s_["gsum_ready"], 1)
                    dve.wait_ge(s_["gsum_ready"], T * b + t + 1)
                    nc.vector.scalar_tensor_tensor(out=heads(cen[:, t, :]), in0=spread(gsum[:, hs].unsqueeze(2), 2, S),
                                                   scalar=-1.0 / S, in1=heads(bank), op0=ALU.mult,
                                                   op1=ALU.add).then_inc(s_["cen_ready"], 1)
                return run

            def b_var(t):
                def run(b, par, n):
                    dve.wait_ge(s_["sq_ready"], T * b + t + 1)
                    nc.vector.tensor_reduce(gvar[:, t * H:(t + 1) * H], heads(sq[:, t, :]), AX.X,
                                            ALU.add).then_inc(s_["gvar_ready"], 1)
                return run

            def b_root(b, par, n):
                dve.wait_ge(s_["gvar_ready"], T * b + T)
                root(b)

            def b_nrm(t):
                def run(b, par, n):
                    cen3 = heads(cen[:, t, :])
                    nc.vector.tensor_tensor(cen3, cen3, spread(grs[:, t * H:(t + 1) * H].unsqueeze(2), 2, S),
                                            ALU.mult).then_inc(s_["nrm_ready"], 1)
                return run

            def b_gn(b, par, n):
                dve.wait_ge(s_["y1_ready"], b + 1)
                dve.wait_ge(s_["g_ready"], b + 1)
                yf = yb.rearrange("p c l -> p (c l)")
                nc.vector.scalar_tensor_tensor(out=yf, in0=yf, scalar=0.5, in1=gT[:, par, :], op0=ALU.mult,
                                               op1=ALU.mult).then_inc(s_["y_ready"], 1)

            def b_wo(t):
                def run(b, par, n):
                    dve.wait_ge(s_["wo_ready"], T * b + t + 1)
                    nc.vector.tensor_tensor(x1[:, t, :], BA[:, t * E:(t + 1) * E], xt[:, par, t, :],
                                            ALU.add).then_inc(s_["x1_ready"], 1)
                    dve.wait_ge(s_["x1_ready"], T * b + t + 1)
                    stats(x1, st2, s_["st2_ready"], mv2, s_["mv2_ready"], T * b + t, [t])
                return run

            def b_xhat2(t):
                def run(b, par, n):
                    dve.wait_ge(s_["rs2_ready"], T * b + t + 1)
                    norm(xhat2, x1, mv2, rs2, [t]).then_inc(s_["xhat2_ready"], 1)
                return run

            def b_norm2(b, par, n):
                dve.wait_ge(s_["xn2T_ready"], b + 1)
                nc.vector.tensor_tensor(sx2, xn2T[:, :, 0:L], xn2T[:, :, 1:L + 1],
                                        ALU.subtract).then_inc(s_["sx2_ready"], 1)
                dve.wait_ge(s_["sx2_ready"], b + 1)
                for dst, at, ready in ((xk, FFN_MAA_K, "xk_ready"), (xr, FFN_MAA_R, "xr_ready")):
                    for c in range(C):
                        ins = nc.vector.scalar_tensor_tensor(out=dst[:, c, :], in0=sx2[:, c, :],
                                                             scalar=cols_s[:, c, at:at + 1],
                                                             in1=xn2T[:, c, 1:L + 1], op0=ALU.mult, op1=ALU.add)
                    ins.then_inc(s_[ready], 1)

            def b_out(t):
                def run(b, par, n):
                    dve.wait_ge(s_["rr_ready"], b + 1)
                    dve.wait_ge(s_["fv_ready"], T * b + t + 1)
                    nc.vector.scalar_tensor_tensor(out=rr[:, t, :], in0=rr[:, t, :], scalar=1.0,
                                                   in1=FA[:, t * E:(t + 1) * E], op0=ALU.add,
                                                   op1=ALU.mult).then_inc(s_["mul_ready"], 1)
                    dve.wait_ge(s_["mul_ready"], T * b + t + 1)
                    nc.vector.scalar_tensor_tensor(out=outt[:, t, :], in0=rr[:, t, :], scalar=0.5, in1=x1[:, t, :],
                                                   op0=ALU.mult, op1=ALU.add).then_inc(s_["out_ready"], 1)
                return run

            steps = dict(f_stats=f_stats, f_norm=f_norm, f_xin=f_xin, b_gate=b_gate, b_root=b_root, b_gn=b_gn,
                         b_norm2=b_norm2)
            for t in range(T):
                steps.update({f"b_o{t}": b_o(t), f"b_cen{t}": b_cen(t), f"b_var{t}": b_var(t), f"b_nrm{t}": b_nrm(t),
                              f"b_wo{t}": b_wo(t), f"b_xhat2{t}": b_xhat2(t), f"b_out{t}": b_out(t)})
            steps.update({f"f_mix{j}": f_mix(j) for j in range(NMIX)})
            steps.update({f"b_mul{i}": b_mul(i) for i in range(ND)})
            steps.update({f"b_red{i}": b_red(i) for i in range(2, ND)})
            steps.update({f"b_step{m}": b_step(m) for m in (1, 2, 4, 8)})
            steps.update({f"b_ktok{m}": b_ktok(l) for l, m in enumerate(LEVELS)})
            steps.update({f"b_kv{q}": b_kv(q) for q in range(NS)})
            steps.update({f"b_rstep{m}": b_rstep(l) for l, m in enumerate(LEVELS) if m < P})
            walk(dve, steps, ORDER["vector"])


def kernel(**inputs):
    import concourse.bacc as bacc
    from concourse.bass_utils import run_bass_kernel_spmd

    a = {k.replace("L0_xattn_", ""): np.asarray(v) for k, v in inputs.items()}
    ctx = a["ctx_2048"]

    def tiles(w):
        return w.reshape(C, P, -1).transpose(1, 0, 2)

    vectors = np.concatenate([
        a["ln1_w"][None], a["ln1_b"][None], a["ln2_w"][None], a["ln2_b"][None], a["maa_x"][None], a["maa_stack"],
        a["time_decay"][None], a["faaaa"].reshape(1, E), a["gn_w"][None], a["gn_b"][None], a["ffn_maa_k"][None],
        a["ffn_maa_r"][None], ctx[:, 1], ctx[:, 0]])
    p = np.arange(P)
    tokmask = np.stack([(p // m == 2 * i) for m in LEVELS[:3] for i in range(P // (2 * m))], 1)
    arrays = dict(
        x=a["x"],
        cols=tiles(vectors.T),
        s0=ctx[:, 2:2 + S].reshape(B, C, P, S).transpose(2, 0, 1, 3),
        w1=tiles(a["maa_w1"]), w2a=a["maa_w2"][:4].reshape(P, E), w2b=a["maa_w2"][4],
        dw1=tiles(a["decay_w1"]), dw2=a["decay_w2"],
        wk=tiles(a["Wk"].T), wv=tiles(a["Wv"].T), wr=tiles(a["Wr"].T), wg=tiles(a["Wg"].T), wo=tiles(a["Wo"].T),
        fk=tiles(a["ffn_Wk"].T), fr=tiles(a["ffn_Wr"].T), fv=tiles(a["ffn_Wv"].T),
        ident=np.eye(P, dtype=np.float32),
        headmask=(p[:, None] // S == p[None, :] // S).astype(np.float32),
        tokmask=tokmask.astype(np.float32))
    arrays = {k: np.ascontiguousarray(v) for k, v in arrays.items()}
    nc = bacc.Bacc("TRN2", target_bir_lowering=False, num_devices=1)
    args = [nc.dram_tensor(k, v.shape, mybir.dt.from_np(v.dtype), kind="ExternalInput").ap()
            for k, v in arrays.items()]
    args.append(nc.dram_tensor("out", (B, L, E), F32, kind="ExternalOutput").ap())
    wkv_kernel(nc, *args)
    r = run_bass_kernel_spmd(nc, [arrays], core_ids=[0])
    return r.results[0]["out"]
```
